# Optimizing a Trainium2 kernel written in Bass

```python
import numpy as np
import jax
import jax.numpy as jnp

def _softmax(x, axis=-1):
    return jax.nn.softmax(x, axis=axis)

def _gelu(x):
    return jax.nn.gelu(x, approximate=True)

def _silu(x):
    return jax.nn.silu(x)

def _sigmoid(x):
    return jax.nn.sigmoid(x)

def _layernorm(x, axis=-1, eps=1e-05):
    m = jnp.mean(x, axis=axis, keepdims=True)
    v = jnp.var(x, axis=axis, keepdims=True)
    return (x - m) / jnp.sqrt(v + eps)

def _scatter_add(tgt, idx, src, axis=0):
    return tgt.at[idx].add(src)

def _segment_sum(src, seg, n):
    return jax.ops.segment_sum(src, seg, n)
kernel_name = 'mk_gnn_preln_d2_gnn_r16_e65abf'

def setup_inputs(seed: int=0):
    np.random.seed(seed)
    _w = jnp.asarray

    def _rec_inputs():
        import jax
        import jax.numpy as jnp
        _gk = jax.random.key(seed)
        x = -0.000202 + 1 * jax.random.normal(jax.random.fold_in(_gk, 1), (3125, 128), jnp.float32)
        _s = jax.random.randint(jax.random.fold_in(_gk, 2), (50000,), 0, 3125, jnp.int32)
        _d = jax.random.randint(jax.random.fold_in(_gk, 3), (50000,), 0, 3125, jnp.int32)
        _loop = jnp.arange(3125, dtype=jnp.int32)
        src = jnp.concatenate([_s, _d, _loop])
        dst = jnp.concatenate([_d, _s, _loop])
        _o = jnp.argsort(dst, stable=True)
        src = src[_o]
        dst = dst[_o]
        edge_type_4 = jax.random.randint(jax.random.fold_in(_gk, 14), (103125,), 0, 4, jnp.int32)
        return (x, src, dst, edge_type_4)
    x, src, dst, edge_type_4 = _rec_inputs()

    def _L0_gnn_setup():
        import jax, jax.numpy as jnp
        import numpy as np
        N_NODES = 3125
        N_EDGES = 37500
        IN_DIM = 128
        HOP_NUM = 10
        ALPHA = 0.1
        key = jax.random.key(seed)
        k_h, k_d, k_r, k_src, k_dst = jax.random.split(key, 5)
        h = jax.random.normal(k_h, (N_NODES, IN_DIM), dtype=jnp.float32)
        d = jax.random.uniform(k_d, (N_NODES,), dtype=jnp.float32)
        layer_reg = jax.random.uniform(k_r, (HOP_NUM,), dtype=jnp.float32)
        src = jax.random.randint(k_src, (N_EDGES,), 0, N_NODES, dtype=jnp.int64)
        dst = jax.random.randint(k_dst, (N_EDGES,), 0, N_NODES, dtype=jnp.int64)
        return {'h': h, 'd': d, 'layer_reg': layer_reg, 'src': src, 'dst': dst}
    _L0_gnn_all = _L0_gnn_setup()
    _L0_gnn_in = {k: v for k, v in _L0_gnn_all.items() if k in ('layer_reg',)}
    del _L0_gnn_all

    def _L1_gnn_setup():
        import jax, jax.numpy as jnp
        import numpy as np
        N_NODES = 3125
        N_EDGES = 37500
        DIM = 128
        N_EDGE_TYPES = 4
        N_STEPS = 4

        def _gru_cell(x, h, w_ih, w_hh, b_ih, b_hh):
            gi = x @ w_ih.T + b_ih
            gh = h @ w_hh.T + b_hh
            i_r, i_z, i_n = jnp.split(gi, 3, axis=-1)
            h_r, h_z, h_n = jnp.split(gh, 3, axis=-1)
            r = jax.nn.sigmoid(i_r + h_r)
            z = jax.nn.sigmoid(i_z + h_z)
            n = jnp.tanh(i_n + r * h_n)
            return (1.0 - z) * n + z * h

        def _step(embedding, src, dst, etype, W_msg, b_msg, w_ih, w_hh, b_ih, b_hh):
            n = embedding.shape[0]
            m = (embedding @ W_msg.T + b_msg).reshape(n, N_EDGE_TYPES, DIM)
            q = m[src, etype]
            r = jax.ops.segment_sum(q, dst, num_segments=n)
            return _gru_cell(r, embedding, w_ih, w_hh, b_ih, b_hh)
        key = jax.random.key(seed)
        ks = jax.random.split(key, 9)
        bound = 1.0 / np.sqrt(DIM)
        return {'embedding': jax.random.normal(ks[0], (N_NODES, DIM), dtype=jnp.float32), 'edge_uv': jax.random.randint(ks[1], (2, N_EDGES), 0, N_NODES, dtype=jnp.int64), 'edge_type': jax.random.randint(ks[2], (N_EDGES,), 0, N_EDGE_TYPES, dtype=jnp.int64), 'W_msg': jax.random.uniform(ks[3], (DIM * N_EDGE_TYPES, DIM), jnp.float32, -bound, bound), 'b_msg': jax.random.uniform(ks[4], (DIM * N_EDGE_TYPES,), jnp.float32, -bound, bound), 'w_ih': jax.random.uniform(ks[5], (3 * DIM, DIM), jnp.float32, -bound, bound), 'w_hh': jax.random.uniform(ks[6], (3 * DIM, DIM), jnp.float32, -bound, bound), 'b_ih': jax.random.uniform(ks[7], (3 * DIM,), jnp.float32, -bound, bound), 'b_hh': jax.random.uniform(ks[8], (3 * DIM,), jnp.float32, -bound, bound)}
    _L1_gnn_all = _L1_gnn_setup()
    _L1_gnn_in = {k: v for k, v in _L1_gnn_all.items() if k in ('W_msg', 'b_msg', 'w_ih', 'w_hh', 'b_ih', 'b_hh')}
    del _L1_gnn_all
    return {'x': x, 'src': src, 'dst': dst, 'edge_type_4': edge_type_4, 'L0_gnn_layer_reg': _L0_gnn_in['layer_reg'], 'L1_gnn_W_msg': _L1_gnn_in['W_msg'], 'L1_gnn_b_msg': _L1_gnn_in['b_msg'], 'L1_gnn_w_ih': _L1_gnn_in['w_ih'], 'L1_gnn_w_hh': _L1_gnn_in['w_hh'], 'L1_gnn_b_ih': _L1_gnn_in['b_ih'], 'L1_gnn_b_hh': _L1_gnn_in['b_hh']}

def reference(x, src, dst, edge_type_4, L0_gnn_layer_reg, L1_gnn_W_msg, L1_gnn_b_msg, L1_gnn_w_ih, L1_gnn_w_hh, L1_gnn_b_ih, L1_gnn_b_hh):
    import jax
    import jax.numpy as jnp

    def _L0_gnn_ref(h, d, layer_reg, src, dst):
        import jax, jax.numpy as jnp
        import numpy as np
        N_NODES = 3125
        N_EDGES = 37500
        IN_DIM = 128
        HOP_NUM = 10
        ALPHA = 0.1
        e = d[dst] * d[src]
        feat = h
        for i in range(HOP_NUM):
            msg = feat[src] * e[:, None]
            agg = jax.ops.segment_sum(msg, dst, num_segments=N_NODES)
            feat_p = agg * (1.0 - ALPHA) + ALPHA * h
            r = layer_reg[i]
            feat = feat_p * r + (1.0 - r) * feat
        return feat

    def _L1_gnn_ref(embedding, edge_uv, edge_type, W_msg, b_msg, w_ih, w_hh, b_ih, b_hh):
        import jax, jax.numpy as jnp
        import numpy as np
        N_NODES = 3125
        N_EDGES = 37500
        DIM = 128
        N_EDGE_TYPES = 4
        N_STEPS = 4

        def _gru_cell(x, h, w_ih, w_hh, b_ih, b_hh):
            gi = x @ w_ih.T + b_ih
            gh = h @ w_hh.T + b_hh
            i_r, i_z, i_n = jnp.split(gi, 3, axis=-1)
            h_r, h_z, h_n = jnp.split(gh, 3, axis=-1)
            r = jax.nn.sigmoid(i_r + h_r)
            z = jax.nn.sigmoid(i_z + h_z)
            n = jnp.tanh(i_n + r * h_n)
            return (1.0 - z) * n + z * h

        def _step(embedding, src, dst, etype, W_msg, b_msg, w_ih, w_hh, b_ih, b_hh):
            n = embedding.shape[0]
            m = (embedding @ W_msg.T + b_msg).reshape(n, N_EDGE_TYPES, DIM)
            q = m[src, etype]
            r = jax.ops.segment_sum(q, dst, num_segments=n)
            return _gru_cell(r, embedding, w_ih, w_hh, b_ih, b_hh)
        src, dst = (edge_uv[0], edge_uv[1])
        for _ in range(N_STEPS):
            embedding = _step(embedding, src, dst, edge_type, W_msg, b_msg, w_ih, w_hh, b_ih, b_hh)
        return embedding
    edge_index = jnp.stack([src, dst])
    deg = jnp.maximum(jax.ops.segment_sum(jnp.ones(dst.shape, jnp.float32), dst, num_segments=3125), 1.0)
    deg_isqrt = deg ** (-0.5)
    h = jnp.maximum(_layernorm(x, axis=-1), 0.0)
    x = x + _L0_gnn_ref(h, deg_isqrt, L0_gnn_layer_reg, src, dst)
    h = jnp.maximum(_layernorm(x, axis=-1), 0.0)
    x = x + _L1_gnn_ref(h, edge_index, edge_type_4, L1_gnn_W_msg, L1_gnn_b_msg, L1_gnn_w_ih, L1_gnn_w_hh, L1_gnn_b_ih, L1_gnn_b_hh)
    return x

_drawn_inputs = setup_inputs


def setup_inputs(seed=0):
    import zlib

    import numpy as np

    out = dict(_drawn_inputs(seed))
    spreads = {}
    factors = {}
    for name, (base, spread) in spreads.items():
        noise = np.random.default_rng([zlib.crc32(name.encode()), seed]).standard_normal(out[name].shape)
        drawn = base * np.exp(spread * noise) if base else spread * noise
        out[name] = jnp.asarray(drawn.astype(out[name].dtype))
    for name, factor in factors.items():
        out[name] = (out[name] * factor).astype(out[name].dtype)
    return out
```

```python
from contextlib import ExitStack

import numpy as np
import concourse.bass as bass
from concourse import mybir

DT = mybir.dt
F32, F16, F8, I32, U8 = DT.float32, DT.float16, DT.float8e4, DT.int32, DT.uint8
ALU = mybir.AluOpType
ACT = mybir.ActivationFunctionType
AX = mybir.AxisListType
ds = bass.ds

N = 3125
E = 103125
F = 128
TILES = 25
Q = N // TILES
CH = 125
NCH = E // CH
ROWS = 75
PER = NCH // ROWS
W = 8
QB = Q + 1
PAD = NCH + W + 7
CA = TILES * TILES
TYPES = 4
HOPS = 10
STEPS = 4
ALPHA = 0.1
EPS = 1e-5
ONE = 1024
UNIT = 512.0
BOUND = 11.4
MAGIC = 12582912.0
SIZES = [4, 4, 4, 4, 3, 3, 3]
START = [sum(SIZES[:k]) for k in range(7)]
BLOCKS = len(SIZES)
BLOCK_OF = [k for k, n in enumerate(SIZES) for _ in range(n)]
RING = 5
PS0 = 12
DIGITS = 5
LOADS = (TYPES + 1) * DIGITS
BIG = CA * 128
TILE_BYTES = TILES * 128
LO, MANY, LOWBITS = 0, QB, 0x03030303


class Chain:

    def __init__(self, eng, sem):
        self.eng, self.sem, self.base, self.k = eng, sem, 0, 0

    def __call__(self, ins):
        self.k += 1
        ins.then_inc(self.sem, 1)
        self.eng.wait_ge(self.sem, self.base + self.k)

    def loop(self, i, per):
        self.start, self.per = self.base + self.k, per
        self.base, self.k = self.start + i * per, 0

    def done(self, count):
        assert self.k == self.per, (self.k, self.per)
        self.base, self.k = self.start + count * self.per, 0


def build(nc, x, src, dst, edge_type, layer_reg, w_msg, b_msg, w_ih, w_hh, b_ih, b_hh, out):
    scr_mm = nc.dram_tensor("chunk_minmax", (2, NCH), F32).ap()
    scr_win = nc.dram_tensor("windows", (2, QB), I32).ap()
    packed_dram = nc.dram_tensor("packed_counts", (128, BIG), U8).ap()
    x2_dram = nc.dram_tensor("x_after_hops", (Q, TILES * F), F32).ap()
    digits_dram = nc.dram_tensor("digit_counts", (LOADS, 128, BIG), U8).ap()

    ctx = ExitStack()
    with ctx:
        def sb(name, shape, dt, where=None):
            return (where or ctx).enter_context(nc.sbuf_tensor(name, shape, dt))

        def sem(name):
            return ctx.enter_context(nc.semaphore(name))

        big1 = sb("big1", [128, BIG], U8)
        tot = big1[:, :].rearrange("p (c a q) -> p c a q", c=TILES, a=TILES)
        tot_f8 = big1[:, :].bitcast(F8).rearrange("p (c a q) -> p c a q", c=TILES, a=TILES)
        ident = sb("ident", [128, 128], F32)
        wt_msg = sb("wt_msg", [128, TYPES * F], F32)
        wt_ih = sb("wt_ih", [128, 3 * F], F32)
        wt_hh = sb("wt_hh", [128, 3 * F], F32)
        bias_msg = sb("bias_msg", [128, TYPES * F], F32)
        bias_ih = sb("bias_ih", [128, 3], F32)
        bias_hh = sb("bias_hh", [128, 3], F32)
        bias_rz = sb("bias_rz", [128, 2], F32)
        bias_nat = sb("bias_nat", [128, TYPES], F32)
        reg = sb("reg", [128, HOPS + 1], F32)
        keep = sb("keep", [128, HOPS + 1], F32)
        anchor = sb("anchor", [128, HOPS + 1], F32)
        grow = sb("grow", [128, 2, HOPS], F32)
        bnd = sb("bnd", [128, HOPS + 1], F32)
        expo = sb("expo", [128, HOPS + 1], I32)
        scale = sb("scale", [128, HOPS + 1], I32)
        unscale = sb("unscale", [128, HOPS + 1], I32)
        gain = sb("gain", [128, HOPS], F32)
        coef = sb("coef", [128, TILES], F32)
        mbound = sb("mbound", [128, 8], F32)
        mexp = sb("mexp", [128, 3], I32)
        mscale = sb("mscale", [128, 2], F32)
        deg = sb("deg", [128, TILES], F32)
        inv_deg = sb("inv_deg", [128, TILES], F32)
        dis = sb("dis", [128, TILES], F32)
        sqd = sb("sqd", [128, TILES], F32)
        stat6 = sb("stat6", [128, 2, 6], F32)
        stats = sb("stats", [128, TILES, 2], F32)
        rs = sb("rs", [128, 4, TILES], F32)
        over = sb("over", [128, QB], F32)
        over1 = sb("over1", [128, 2], F32)
        neg_lim = sb("neg_lim", [128, 1], F32)
        windows = sb("windows_row", [1, 2 * QB], I32)
        flag = sb("flag", [1, 1], I32)
        scrap = sb("scrap", [128, 1], I32)
        ones16 = sb("ones16", [128, 128], F16)
        onesf = sb("onesf", [128, 1], F32)
        hd = sb("hd", [128, TILES, F], F32)

        with ExitStack() as b:
            keys = sb("keys", [128, PAD], F32, b)
            tab = sb("tab", [128, 2, PAD], F16, b)
            win = sb("win", [128, 2, 2, W], F32, b)
            win_p = sb("win_p", [128, 2, W], F16, b)
            win_x = sb("win_x", [128, 3], F32, b)
            hot_pair = sb("hot_pair", [128, W + 1, CA + 1], F16, b)
            hot_place = sb("hot_place", [128, 2, 128, W], F16, b)
            hot_place_x = sb("hot_place_x", [128, 128], F16, b)
            iota_pair = sb("iota_pair", [128, CA + 1], F16, b)
            iota_place = sb("iota_place", [128, 128, W], F16, b)
            q_off = sb("q_off", [128, QB], F32, b)
            sums = sb("sums", [128, CA], DT.uint16, b)
        with ExitStack() as b:
            g = sb("g", [128, TILES, F], F32, b)
            parts0 = sb("parts0", [128, TILES, 2, F], F16, b)
            hop_tmp = sb("hop_tmp", [128, 3, F], F32, b)
        with ExitStack() as b:
            r_t = sb("r_t", [128, 2, 512], F32, b)
            gate_r = sb("gate_r", [128, 512], F32, b)
            gate_z = sb("gate_z", [128, 512], F32, b)
            cand_h = sb("cand_h", [128, 512], F32, b)
            cand_t = sb("cand_t", [128, 512], F32, b)
            cand = sb("cand", [128, 512], F32, b)
            diff = sb("diff", [128, 512], F32, b)
            m_full = sb("m_full", [128, 2, 512], F32, b)
        emb = hd[:, :, 0:Q]

        sb("shared_room", [128, 27 * 1024 + 64], U8)

        with ExitStack() as b:
            big2 = sb("big2", [128, BIG], U8, b)
        packed = big2[:, :].rearrange("p (c a q) -> p c a q", c=TILES, a=TILES)
        with ExitStack() as b:
            edge_i = sb("edge_i", [128, 3, PER * CH], I32, b)
            edge_f = sb("edge_f", [128, 3, PER * CH], F32, b)
            edge_p = sb("edge_p", [128, 3, PER * CH], F32, b)
            edge_t = sb("edge_t", [128, PER * CH], F32, b)
            mm = sb("mm", [128, 2, PER], F32, b)
            mmb = sb("mmb", [128, 2, NCH], F32, b)
            chunk = sb("chunk", [128, NCH], F32, b)
            hit = sb("hit", [128, 2, NCH], F32, b)
            lohi = sb("lohi", [128, 4], F32, b)
            win_i = sb("win_i", [128, 2], I32, b)
            q25 = sb("q25", [128, 2], F32, b)
        with ExitStack() as b:
            parts1 = sb("parts1", [128, TILES, 2, F], F16, b)
            x_again = sb("x_again", [128, TILES, F], F32, b)
            x2 = sb("x2", [128, TILES, F], F32, b)
            normed = sb("normed", [128, TILES, F], F32, b)
        with ExitStack() as b:
            m_parts = sb("m_parts", [128, TILES, 2, TYPES * F], F16, b)
            slots = sb("slots", [128, 2, 4 * TILES * 128], U8, b)
        tile_u8 = big1[:, 0:TYPES * DIGITS * TILE_BYTES].rearrange("p (l n) -> p l n", n=TILE_BYTES)
        tile_f8 = tile_u8.bitcast(F8).rearrange("p l (a q) -> p l a q", q=128)
        with ExitStack() as b:
            cnt_i = sb("cnt_i", [128, 2, CA], I32, b)
            cnt_m = sb("cnt_m", [128, CA], I32, b)
            cnt_8 = sb("cnt_8", [128, CA], F8, b)
            want = sb("want", [128, TYPES + 1], F32, b)
            every = sb("every", [128, TYPES + 1], F32, b)
            mask = sb("mask", [128, DIGITS], I32, b)
        slots_f8 = slots[:, :, :].bitcast(F8).rearrange("p s (c a q) -> p s c a q", c=4, a=TILES)
        x_raw = big1[:, 0:TILES * F * 4].bitcast(F32).rearrange("p (c f) -> p c f", c=TILES)
        w_raw = big1[:, 16384:16384 + 10 * F * 4].bitcast(F32).rearrange("p (t f) -> p t f", t=10)
        x2_back = x_raw
        result = big1[:, 16384:16384 + TILES * F * 4].bitcast(F32).rearrange("p (c f) -> p c f", c=TILES)

        ps = ctx.enter_context(nc.psum_tensor("ps", [128, 8, 512], F32))
        junk = [ps[:, 2 * i + 4:2 * i + 6, :].rearrange("p b n -> p (b n)")[:, PS0:PS0 + CA] for i in range(2)]
        pairs = [ps[:, 2 * i:2 * i + 2, :].rearrange("p b n -> p (b n)")[:, PS0:PS0 + CA] for i in range(2)]

        s_edges, s_x, s_raw, s_small = sem("edges_loaded"), sem("x_loaded"), sem("weights_loaded"), sem("small_loaded")
        s_const = sem("constants_made")
        s_dve, s_dve_late = sem("vector_steps"), sem("late_vector_steps")
        s_mm, s_mm_out, s_mm_in = sem("minmax_made"), sem("minmax_stored"), sem("minmax_loaded")
        s_key, s_tr, s_trc = sem("edge_rows_made"), sem("edge_rows_transposed"), sem("tables_made")
        s_win, s_win_out, s_win_in = sem("windows_made"), sem("windows_stored"), sem("windows_loaded")
        s_wtr = sem("weights_transposed")
        s_bnd, s_bndr = sem("message_bound_made"), sem("message_bound_shared")
        s_sq, s_sqr = sem("variance_made"), sem("root_made")
        s_prep = sem("staging_free")
        s_wst, s_hot, s_hot_used = sem("window_staged"), sem("onehots_made"), sem("onehots_used")
        s_xs_g = sem("extra_weighed")
        s_xs, s_more, s_more_used = sem("extra_staged"), sem("extra_made"), sem("extra_used")
        s_taken, s_flagq, s_sums = sem("counts_taken"), sem("excess_noted"), sem("sums_copied_out")
        s_flag, s_flagp, s_flagi = sem("excess_reduced"), sem("excess_summed"), sem("flag_made")
        s_packed = sem("packed_stored")
        s_deg, s_degd = sem("degrees_summed"), sem("degrees_made")
        s_parts, s_acc, s_ring = sem("hop_parts_made"), sem("hop_summed"), sem("hop_bank_free")
        s_pblk = [sem(f"packed_loaded{k}") for k in range(BLOCKS)]
        s_xa, s_x2, s_x2_out = sem("x_loaded_again"), sem("x2_made"), sem("x2_stored")
        s_nrm, s_ntr, s_emb = sem("normed_made"), sem("normed_transposed"), sem("embedding_made")
        s_slot, s_slot_free = sem("slot_unpacked"), sem("slot_used")
        s_m, s_mfull, s_hi, s_mp = sem("messages_made"), sem("messages_copied"), sem("high_parts"), sem("message_parts")
        s_rt = sem("messages_summed")
        s_grz, s_gn, s_sig, s_ct, s_tanh = sem("rz_products"), sem("n_products"), sem("rz_gates"), sem("n_sum"), sem("candidate")
        s_tables = sem("general_tables_made")
        s_plane, s_dve_g = sem("digits_stored"), sem("general_vector_steps")
        s_ld, s_sacc, s_epi = sem("tile_loaded"), sem("tile_summed"), sem("tile_finished")
        s_ld_m, s_sacc_m, s_epi_m = sem("typed_tile_loaded"), sem("typed_tile_summed"), sem("embedding_tile_made")
        s_x2b, s_otr, s_res, s_out = sem("x2_back"), sem("embedding_back"), sem("result_made"), sem("out_stored")

        block = ctx.enter_context(nc.Block())

        x_v = x.rearrange("(p t) f -> p (t f)", t=TILES)
        out_v = out.rearrange("(p t) f -> p (t f)", t=TILES)

        @block.sync
        def _(sp):
            for j, a in enumerate((dst, src, edge_type)):
                sp.dma_start(edge_i[0:ROWS, j, :], a.rearrange("(p e) -> p e", p=ROWS)).then_inc(s_edges, 16)
            sp.wait_ge(s_mm, 1)
            sp.dma_start(scr_mm.rearrange("s (p k) -> p s k", p=ROWS), mm[0:ROWS, :, :]).then_inc(s_mm_out, 16)
            sp.wait_ge(s_mm_out, 16)
            sp.dma_start(mmb[0:QB, :, :], scr_mm.partition_broadcast(QB)).then_inc(s_mm_in, 16)
            sp.wait_ge(s_win, 1)
            with nc.allow_non_contiguous_dma("126 x 2 words"):
                sp.dma_start(scr_win.rearrange("s q -> q s"), win_i[0:QB, :]).then_inc(s_win_out, 16)
            sp.wait_ge(s_win_out, 16)
            sp.dma_start(windows[0:1, :], scr_win.rearrange("(o s) q -> o (s q)", o=1)).then_inc(s_win_in, 16)
            sp.wait_ge(s_taken, QB + 2)
            for k in range(5):
                sp.dma_start(packed_dram[:, k * BIG // 5:(k + 1) * BIG // 5],
                             big2[:, k * BIG // 5:(k + 1) * BIG // 5]).then_inc(s_packed, 16)
            sp.wait_ge(s_flagi, 1)
            over_any = sp.value_load(flag[0:1, 0:1], min_val=0, max_val=1)
            sp.wait_ge(s_packed, 80)
            sp.dma_start(x_again[0:Q, :, :].rearrange("p c f -> p (c f)"), x_v).then_inc(s_xa, 16)
            with sp.If(over_any < 1):
                sp.wait_ge(s_acc, HOPS * TILES)
                for k in range(BLOCKS):
                    a, z = START[k] * TILE_BYTES, (START[k] + SIZES[k]) * TILE_BYTES
                    sp.dma_start(big1[:, a:z], packed_dram[:, a:z]).then_inc(s_pblk[k], 16)
            sp.wait_ge(s_x2, 1)
            sp.dma_start(x2_dram, x2[0:Q, :, :].rearrange("p c f -> p (c f)")).then_inc(s_x2_out, 16)
            sp.wait_ge(s_x2_out, 16)
            with sp.If(over_any > 0):
                sp.wait_ge(s_sacc_m, TILES * STEPS + 1)
            with sp.If(over_any < 1):
                sp.wait_ge(s_slot, STEPS * BLOCKS * TYPES)
            sp.dma_start(x2_back[0:Q, :, :].rearrange("p c f -> p (c f)"), x2_dram).then_inc(s_x2b, 16)
            for k in range(BLOCKS):
                a, z = START[k] * F, (START[k] + SIZES[k]) * F
                sp.wait_ge(s_res, k + 1)
                sp.dma_start(out_v[:, a:z], result[0:Q, :, :].rearrange("p c f -> p (c f)")[:, a:z]).then_inc(s_out, 16)
            sp.wait_ge(s_out, 16 * BLOCKS)

        @block.gpsimd
        def _(pool):
            pool.memset(ident[:, :], 0.0).then_inc(s_const, 1)
            pool.wait_ge(s_const, 1)
            pool.affine_select(out=ident[:, :], in_=ident[:, :], compare_op=ALU.not_equal, fill=1.0, base=0,
                               pattern=[[-1, 128]], channel_multiplier=1).then_inc(s_const, 1)
            pool.iota(chunk[:, :], [[1, NCH]], base=0, channel_multiplier=0,
                      allow_small_or_imprecise_dtypes=True).then_inc(s_const, 1)
            pool.iota(q25[:, :], [[TILES - 1, 2]], base=0, channel_multiplier=TILES,
                      allow_small_or_imprecise_dtypes=True).then_inc(s_const, 1)
            pool.iota(iota_pair[:, :], [[1, CA + 1]], base=0, channel_multiplier=0,
                      allow_small_or_imprecise_dtypes=True).then_inc(s_const, 1)
            pool.iota(iota_place[:, :, :], [[1, 128], [0, W]], base=0, channel_multiplier=0,
                      allow_small_or_imprecise_dtypes=True).then_inc(s_const, 1)
            pool.iota(q_off[:, :], [[CA, QB]], base=0, channel_multiplier=0,
                      allow_small_or_imprecise_dtypes=True).then_inc(s_const, 1)
            pool.memset(ones16[:, :], 1.0).then_inc(s_const, 1)
            pool.memset(onesf[:, :], 1.0).then_inc(s_const, 1)
            pool.memset(neg_lim[:, :], 0.5 - 4.0 * ONE).then_inc(s_const, 1)
            pool.wait_ge(s_bnd, 1)
            pool.partition_all_reduce(mbound[:, 6:7], mbound[:, 5:6], 128, bass.bass_isa.ReduceOp.max).then_inc(s_bndr, 1)
            pool.wait_ge(s_trc, 3)
            pool.wait_ge(s_win_in, 16)

            def stage(n, q, b):
                lo = pool.value_load(windows[0:1, ds(q, 1)], min_val=0, max_val=NCH)
                pool.wait_ge(s_hot, W * n + W)
                pool.tensor_tensor(win[0:CH, b, 0, :], keys[0:CH, ds(lo, W)], q_off[0:CH, ds(q, 1)].broadcast_to([CH, W]), ALU.subtract)
                pool.tensor_copy(win[0:CH, b, 1, :], tab[0:CH, 1, ds(lo, W)])
                pool.tensor_copy(win_p[0:CH, b, :], tab[0:CH, 0, ds(lo, W)]).then_inc(s_wst, 1)

            with pool.Fori(0, QB // 2) as i:
                stage(2 * i, 2 * i, 0)
                stage(2 * i + 1, 2 * i + 1, 1)
            pool.wait_ge(s_flagi, 1)
            with pool.If(pool.value_load(flag[0:1, 0:1], min_val=0, max_val=1) > 0):
                with pool.Fori(0, LOADS) as load:
                    with pool.Fori(0, QB // 2) as i:
                        for b in range(2):
                            stage(QB * (load + 1) + 2 * i + b, 2 * i + b, b)
                    pool.wait_ge(s_taken, QB * load + 2 * QB + 2)
                    pool.dma_start(digits_dram[ds(load, 1), :, :].rearrange("o p n -> (o p) n"), big1[:, :]).then_inc(s_plane, 16)
                pool.wait_ge(s_plane, 16 * LOADS)
                with pool.Fori(0, HOPS + 1) as u:
                    with pool.Fori(0, TILES) as c:
                        pool.wait_ge(s_sacc, TILES * u + c + 1)
                        for d in range(DIGITS):
                            pool.dma_start(tile_u8[:, d, :], digits_dram[TYPES * DIGITS + d, :, ds(c * TILE_BYTES, TILE_BYTES)])\
                                .then_inc(s_ld, 16)
                pool.wait_ge(s_sacc, TILES * (HOPS + 1) + 1)
                with pool.Fori(0, STEPS) as s:
                    with pool.Fori(0, TILES) as c:
                        pool.wait_ge(s_sacc_m, TILES * s + c + 1)
                        for load in range(TYPES * DIGITS):
                            pool.dma_start(tile_u8[:, load, :], digits_dram[load, :, ds(c * TILE_BYTES, TILE_BYTES)])\
                                .then_inc(s_ld_m, 16)
                pool.wait_ge(s_ld_m, 16 * TYPES * DIGITS * TILES * STEPS)

        @block.scalar
        def _(act):
            act.dma_start(x_raw[0:Q, :, :].rearrange("p c f -> p (c f)"), x_v).then_inc(s_x, 16)
            act.dma_start(w_raw[:, 0:4, :], w_msg.rearrange("(t j) f -> j t f", t=4)).then_inc(s_raw, 16)
            act.dma_start(w_raw[:, 4:7, :], w_ih.rearrange("(t j) f -> j t f", t=3)).then_inc(s_raw, 16)
            act.dma_start(w_raw[:, 7:10, :], w_hh.rearrange("(t j) f -> j t f", t=3)).then_inc(s_raw, 16)
            act.dma_start(bias_msg[:, :], b_msg.partition_broadcast(128)).then_inc(s_small, 16)
            act.dma_start(reg[:, 0:HOPS], layer_reg.partition_broadcast(128)).then_inc(s_small, 16)
            with nc.allow_non_contiguous_dma("biases by gate"):
                act.dma_start(bias_ih[:, :], b_ih.rearrange("(g p) -> p g", p=128)).then_inc(s_small, 16)
                act.dma_start(bias_hh[:, :], b_hh.rearrange("(g p) -> p g", p=128)).then_inc(s_small, 16)
                act.dma_start(bias_nat[:, :], b_msg.rearrange("(g p) -> p g", p=128)).then_inc(s_small, 16)

            def root(n):
                act.wait_ge(s_sq, n)
                act.activation(rs[0:Q, 1, :], rs[0:Q, 0, :], ACT.Sqrt).then_inc(s_sqr, 1)

            root(1)
            act.wait_ge(s_prep, 1)

            act.wait_ge(s_const, 10)
            act.wait_ge(s_win_in, 16)
            act.sem_inc(s_flagq, 2)
            act.sem_inc(s_rt, 1)
            act.sem_inc(s_sig, 1)
            extras = act.alloc_register("extras_expected")
            act.reg_mov(extras, 1)

            def summed(n, q):
                act.wait_ge(s_hot_used, W * n + 2 * W)
                act.reg_add(extras, extras, act.value_load(windows[0:1, ds(q + MANY, 1)], min_val=0, max_val=NCH))
                act.wait_ge(s_more_used, act.snap(extras))
                act.wait_ge(s_flagq, n + 1)

            def evacuate(q, b):
                summed(q, q)
                by_q = [m[:, :].rearrange("p (n q) -> p n q", q=128)[:, :, ds(q, 1)].rearrange("p n q -> p (n q)")
                        for m in (big1, big2)]
                act.activation(by_q[0], pairs[b], ACT.Copy, scale=1.0 / ONE)
                act.wait_ge(s_taken, q + 2)
                act.activation(sums[:, :], pairs[b], ACT.Copy).then_inc(s_sums, 1)
                act.activation(junk[b], pairs[b], ACT.Relu, bias=neg_lim[:, 0:1],
                               accum_out=over[:, ds(q, 1)]).then_inc(s_flagq, 1)
                act.wait_ge(s_sums, q + 1)
                act.activation(by_q[1], sums[:, :].bitcast(U8).rearrange("p (n two) -> p n two", two=2)[:, :, 0],
                               ACT.Copy).then_inc(s_taken, 1)

            with act.Fori(0, QB // 2) as i:
                evacuate(2 * i, 0)
                evacuate(2 * i + 1, 1)
            act.wait_ge(s_flagi, 1)
            over_any = act.value_load(flag[0:1, 0:1], min_val=0, max_val=1)
            with act.If(over_any > 0):
                act.wait_ge(s_tables, 1)
                with act.Fori(0, LOADS) as load:
                    with act.Fori(0, QB // 2) as i:
                        for b in range(2):
                            n = QB * (load + 1) + 2 * i + b
                            summed(n, 2 * i + b)
                            act.wait_ge(s_taken, n + 1)
                            act.activation(cnt_i[:, b, :], pairs[b], ACT.Copy).then_inc(s_flagq, 1)
            root(2)
            root(3)
            for k in range(BLOCKS):
                act.wait_ge(s_ntr, k + 1)
                act.activation(emb[:, START[k]:START[k] + SIZES[k], :],
                               ps[:, k, 0:SIZES[k] * Q].rearrange("p (c q) -> p c q", q=Q), ACT.Relu).then_inc(s_emb, 1)
            def high(s):
                for a in range(TILES):
                    act.wait_ge(s_mfull, TILES * s + a + 2)
                    act.activation(m_parts[0:Q, a, 0, :], m_full[0:Q, a % 2, :], ACT.Copy).then_inc(s_hi, 1)

            def update(turn, n, bank):
                act.activation(r_t[:, bank, 0:n], ps[:, bank, 0:n], ACT.Copy, scale=mscale[:, 1:2]).then_inc(s_rt, 1)
                act.wait_ge(s_grz, turn + 1)
                act.activation(gate_r[:, 0:n], ps[:, 2, 0:n], ACT.Sigmoid, bias=bias_rz[:, 0:1]).then_inc(s_sig, 1)
                act.activation(gate_z[:, 0:n], ps[:, 3, 0:n], ACT.Sigmoid, bias=bias_rz[:, 1:2]).then_inc(s_sig, 1)
                act.wait_ge(s_ct, turn + 2)
                act.activation(cand[:, 0:n], cand_t[:, 0:n], ACT.Tanh, bias=bias_ih[:, 2:3]).then_inc(s_tanh, 1)

            with act.If(over_any > 0):
                with act.Fori(0, STEPS) as s:
                    high(s)
                    with act.Fori(0, TILES) as c:
                        act.wait_ge(s_sacc_m, TILES * s + c + 2)
                        update(TILES * s + c, Q, 0)
            with act.If(over_any < 1):
                with act.Fori(0, STEPS) as s:
                    high(s)
                    for k in range(BLOCKS):
                        act.wait_ge(s_slot_free, TYPES * (BLOCKS * s + k + 1) + 2)
                        update(BLOCKS * s + k, SIZES[k] * Q, k % 2)

        @block.tensor
        def _(pe):
            def wait_alone(sem, value):
                pe.wait_ge(sem, value)
                pe.ldweights(ones16[:, :], tile_position=(0, 0))

            pe.wait_ge(s_const, 2)
            pe.wait_ge(s_raw, 48)
            for t in range(10):
                last = pe.transpose(ps[:, 6 + t // 4 % 2, t % 4 * F:t % 4 * F + F] if t < 8 else
                                    ps[:, 5, (t - 8) * F:(t - 7) * F], w_raw[:, t, :], ident[:, :])
            last.then_inc(s_wtr, 1)
            for j in range(3):
                pe.wait_ge(s_key, j + 1)
                if j == 2:
                    pe.wait_ge(s_trc, 1)
                for k in range(PER):
                    col = k % 6 * ROWS
                    last = pe.transpose(ps[0:CH, j % 2 * 2 + k // 6, col:col + ROWS],
                                        edge_p[0:ROWS, j, k * CH:(k + 1) * CH], ident[0:ROWS, 0:ROWS])
                last.then_inc(s_tr, 1)
            pe.wait_ge(s_trc, 3)
            pe.wait_ge(s_win_in, 16)

            def count(n, q, b):
                first = ps[:, 2 * b, PS0:512]
                second = ps[:, 2 * b + 1, 0:CA - 512 + PS0]
                pe.wait_ge(s_flagq, n + 1)
                for w in range(W):
                    pe.wait_ge(s_hot, W * n + w + 2 * W + 1)
                    pe.matmul(first, hot_place[0:CH, b, :, w], hot_pair[0:CH, w, 0:512 - PS0],
                              start=w == 0, stop=False, skip_group_check=True)
                    last = pe.matmul(second, hot_place[0:CH, b, :, w], hot_pair[0:CH, w, 512 - PS0:CA],
                                     start=w == 0, stop=w == W - 1, skip_group_check=True)
                    last.then_inc(s_hot_used, 1)
                many = pe.value_load(windows[0:1, ds(q + MANY, 1)], min_val=0, max_val=NCH)
                with pe.If(many > 0):
                    with pe.Fori(0, many):
                        pe.reg_add(extras, extras, 1)
                        pe.wait_ge(s_more, pe.snap(extras))
                        pe.matmul(first, hot_place_x[0:CH, :], hot_pair[0:CH, W, 0:512 - PS0],
                                  start=False, stop=False, skip_group_check=True)
                        pe.matmul(second, hot_place_x[0:CH, :], hot_pair[0:CH, W, 512 - PS0:CA],
                                  start=False, stop=False, skip_group_check=True).then_inc(s_more_used, 1)

            extras = pe.alloc_register("extras_seen")
            pe.reg_mov(extras, 0)
            pe.sem_inc(s_hot_used, W)
            with pe.Fori(0, QB // 2) as i:
                count(2 * i, 2 * i, 0)
                count(2 * i + 1, 2 * i + 1, 1)

            pe.wait_ge(s_flag, 1)
            pe.matmul(ps[0:1, 4, 0:1], over1[:, 0:1], onesf[:, 0:1], start=True, stop=True).then_inc(s_flagp, 1)
            pe.wait_ge(s_flagi, 1)
            over_any = pe.value_load(flag[0:1, 0:1], min_val=0, max_val=1)

            def tile_sum(turn, rhs, bank):
                pe.wait_ge(s_epi, turn + 1)
                wait_alone(s_ld, 16 * DIGITS * (turn + 1))
                for d in range(DIGITS):
                    for a in range(TILES):
                        last = pe.matmul(bank, tile_f8[0:Q, d, a, :], rhs(a), start=d == 0 and a == 0,
                                         stop=d == DIGITS - 1 and a == TILES - 1)
                last.then_inc(s_sacc, 1)

            with pe.If(over_any > 0):
                with pe.Fori(0, LOADS) as load:
                    with pe.Fori(0, QB // 2) as i:
                        for b in range(2):
                            count(QB * (load + 1) + 2 * i + b, 2 * i + b, b)
                pe.sem_inc(s_sacc, 1)
                pe.sem_inc(s_sacc_m, 1)
                with pe.Fori(0, TILES) as c:
                    tile_sum(c, lambda a: ones16[0:Q, 0:1], ps[:, 0, 0:1])
            with pe.If(over_any < 1):
                pe.wait_ge(s_taken, QB + 2)
                for c in range(TILES):
                    for a in range(TILES):
                        last = pe.matmul(ps[:, 6, c:c + 1], tot_f8[0:Q, c, a, :], ones16[0:Q, 0:1],
                                         start=a == 0, stop=a == TILES - 1, skip_group_check=True)
                last.then_inc(s_deg, 1)

            def both(parts, a):
                return parts[0:Q, a, :, :].rearrange("p h f -> p (h f)")

            with pe.If(over_any > 0):
                pe.wait_ge(s_parts, TILES)
                with pe.Fori(0, HOPS // 2) as i:
                    for par, parts in enumerate((parts0, parts1)):
                        with pe.Fori(0, TILES) as c:
                            tile_sum(TILES * (2 * i + par + 1) + c, lambda a: both(parts, a), ps[:, 0, 0:2 * F])
            ready = {0: TILES - 3, TILES - 3: TILES - 2, TILES - 2: TILES - 1, TILES - 1: TILES}
            with pe.If(over_any < 1):
                with pe.Fori(0, HOPS // 2) as i:
                    for n in range(2 * TILES):
                        par, c = divmod(n, TILES)
                        wait_alone(s_ring, 2 * TILES * i + n + 1)
                        for a in range(TILES):
                            if c == 0 and a in ready:
                                wait_alone(s_parts, 2 * TILES * i + par * TILES + ready[a])
                            last = pe.matmul(ps[:, n % RING, 0:2 * F], tot_f8[0:Q, c, a, :],
                                             both((parts0, parts1)[par], a), start=a == 0, stop=a == TILES - 1)
                        last.then_inc(s_acc, 1)

            for k in range(BLOCKS):
                pe.wait_ge(s_nrm, START[k] + SIZES[k])
                for j in range(SIZES[k]):
                    last = pe.transpose(ps[:, k, j * Q:(j + 1) * Q], normed[0:Q, START[k] + j, :], ident[0:Q, 0:Q])
                last.then_inc(s_ntr, 1)
            pe.wait_ge(s_emb, BLOCKS)

            def message(s, a):
                pe.wait_ge(s_mfull, TILES * s + max(a, 1))
                pe.matmul(ps[0:Q, 6 + a % 2, :], emb[:, a, :], wt_msg[:, :], start=True, stop=True).then_inc(s_m, 1)

            def gates(turn, n, bank, e):
                r = r_t[:, bank, 0:n]
                pe.wait_ge(s_rt, turn + 2)
                pe.wait_ge(s_sig, 2 * turn + 1)
                pe.wait_ge(s_ct, turn + 1)
                for j in range(2):
                    pe.matmul(ps[:, 2 + j, 0:n], wt_ih[:, j * F:(j + 1) * F], r, start=True, stop=False)
                    last = pe.matmul(ps[:, 2 + j, 0:n], wt_hh[:, j * F:(j + 1) * F], e, start=False, stop=True)
                last.then_inc(s_grz, 1)
                pe.matmul(ps[:, 4, 0:n], wt_ih[:, 2 * F:3 * F], r, start=True, stop=True)
                pe.matmul(ps[:, 5, 0:n], wt_hh[:, 2 * F:3 * F], e, start=True, stop=True).then_inc(s_gn, 1)

            with pe.If(over_any > 0):
                with pe.Fori(0, STEPS) as s:
                    pe.wait_ge(s_epi_m, TILES * s + 1)
                    for a in range(TILES):
                        message(s, a)
                    wait_alone(s_mp, TILES * s + TILES + 1)
                    with pe.Fori(0, TILES) as c:
                        turn = TILES * s + c
                        pe.wait_ge(s_rt, turn + 1)
                        wait_alone(s_ld_m, 16 * TYPES * DIGITS * (turn + 1))
                        for t in range(TYPES):
                            for d in range(DIGITS):
                                for a in range(TILES):
                                    for h in range(2):
                                        last = pe.matmul(ps[:, 0, 0:Q], m_parts[0:Q, a, h, t * F:(t + 1) * F],
                                                         tile_f8[0:Q, t * DIGITS + d, a, 0:Q],
                                                         start=t == 0 and d == 0 and a == 0 and h == 0,
                                                         stop=t == TYPES - 1 and d == DIGITS - 1 and a == TILES - 1 and h == 1)
                        last.then_inc(s_sacc_m, 1)
                        pe.wait_ge(s_epi_m, turn + 1)
                        gates(turn, Q, 0, emb[:, ds(c, 1), :].rearrange("p c q -> p (c q)"))
                pe.wait_ge(s_epi_m, TILES * STEPS + 1)

            with pe.If(over_any < 1):
                with pe.Fori(0, STEPS) as s:
                    def message_when_ready(a):
                        pe.wait_ge(s_emb, BLOCKS * s + BLOCK_OF[a] + 1)
                        message(s, a)

                    def gather(k, ts, a):
                        for t in ts:
                            for h in range(2):
                                last = pe.matmul(ps[:, k % 2, 0:SIZES[k] * Q], m_parts[0:Q, a, h, t * F:(t + 1) * F],
                                                 slots_f8[0:Q, t % 2, 0:SIZES[k], a, 0:Q],
                                                 start=a == 0 and t == 0 and h == 0,
                                                 stop=a == TILES - 1 and t == TYPES - 1 and h == 1)
                            if a == TILES - 1:
                                last.then_inc(s_slot_free, 1)

                    def block_gates(k):
                        gates(BLOCKS * s + k, SIZES[k] * Q, k % 2, emb[:, START[k]:START[k] + SIZES[k], :])

                    for k in range(BLOCKS):
                        used = TYPES * (BLOCKS * s + k)
                        if k == 0:
                            message_when_ready(0)
                            message_when_ready(1)
                            pe.wait_ge(s_rt, BLOCKS * s + 1)
                            pe.wait_ge(s_slot, used + 2)
                            for a in range(TILES):
                                if a + 2 < TILES:
                                    message_when_ready(a + 2)
                                wait_alone(s_mp, TILES * s + a + 2)
                                gather(k, (0, 1), a)
                            rest = (2, 3)
                        else:
                            pe.wait_ge(s_rt, BLOCKS * s + k)
                            rest = (0, 1, 2, 3)
                        for t in rest:
                            wait_alone(s_slot, used + t + 1)
                            for a in range(TILES):
                                gather(k, (t,), a)
                            if t == 0:
                                block_gates(k - 1)
                    block_gates(BLOCKS - 1)
                pe.wait_ge(s_emb, BLOCKS * (STEPS + 1))

            for k in range(BLOCKS):
                for j in range(SIZES[k]):
                    last = pe.transpose(ps[0:Q, k, j * F:(j + 1) * F], emb[:, START[k] + j, :], ident[:, :])
                last.then_inc(s_otr, 1)

        @block.vector
        def _(dve):
            steps, steps_g = Chain(dve, s_dve), Chain(dve, s_dve_g)

            def step(ins):
                steps(ins)

            TS, STT, TT = dve.tensor_scalar, dve.scalar_tensor_tensor, dve.tensor_tensor

            def rsqrt(value, plus, to, n):
                TS(rs[0:Q, 0, :], value, plus, None, ALU.add).then_inc(s_sq, 1)
                dve.wait_ge(s_sqr, n)
                step(dve.reciprocal(rs[0:Q, 2, :], rs[0:Q, 1, :]))
                step(TT(rs[0:Q, 3, :], rs[0:Q, 2, :], rs[0:Q, 2, :], ALU.mult))
                step(TT(rs[0:Q, 3, :], rs[0:Q, 3, :], rs[0:Q, 0, :], ALU.mult))
                step(TS(rs[0:Q, 3, :], rs[0:Q, 3, :], -0.5, 1.5, ALU.mult, ALU.add))
                step(TT(to, rs[0:Q, 3, :], rs[0:Q, 2, :], ALU.mult))

            dve.memset(keys[:, :], -1e6)
            step(dve.memset(tab[:, :, :], 0.0))
            dve.wait_ge(s_edges, 48)
            for j in range(3):
                last = dve.tensor_copy(edge_f[0:ROWS, j, :], edge_i[0:ROWS, j, :])
            step(last)
            by_chunk = edge_f[0:ROWS, 0, :].rearrange("p (k e) -> p k e", k=PER)
            dve.tensor_reduce(mm[0:ROWS, 0, :], by_chunk, AX.X, ALU.min)
            dve.tensor_reduce(mm[0:ROWS, 1, :], by_chunk, AX.X, ALU.max).then_inc(s_mm, 1)
            target, source, kind = (edge_f[0:ROWS, j, :] for j in range(3))
            key, place, weight = (edge_p[0:ROWS, j, :] for j in range(3))
            tmp = edge_t[0:ROWS, :]
            step(TS(place, source, -float(TILES // 2), 1.0 / TILES, ALU.add, ALU.mult))
            step(TS(place, place, MAGIC, -MAGIC, ALU.add, ALU.add))
            step(STT(out=tmp, in0=place, scalar=-float(TILES), in1=source, op0=ALU.mult, op1=ALU.add))
            STT(out=key, in0=target, scalar=float(TILES), in1=tmp, op0=ALU.mult, op1=ALU.add).then_inc(s_key, 2)
            step(TS(weight, kind, 1.0, 3.0, ALU.is_ge, ALU.mult))
            for t in (2, 3):
                step(TS(tmp, kind, float(t), 3.0 * 4 ** (t - 1), ALU.is_ge, ALU.mult))
                step(TT(weight, weight, tmp, ALU.add))
            TS(weight, weight, ONE + 1.0, None, ALU.add).then_inc(s_key, 1)
            for j in range(3):
                dve.wait_ge(s_tr, j + 1)
                to = (keys[0:CH, :], tab[0:CH, 0, :], tab[0:CH, 1, :])[j][:, 0:NCH].rearrange("e (p k) -> e k p", k=PER)
                for half, (lo, hi) in enumerate(((0, 6), (6, PER))):
                    last = dve.tensor_copy(to[:, lo:hi, :], ps[0:CH, j % 2 * 2 + half, 0:(hi - lo) * ROWS]
                                           .rearrange("e (k p) -> e k p", p=ROWS))
                last.then_inc(s_trc, 1)
            dve.wait_ge(s_mm_in, 16)
            dve.wait_ge(s_const, 10)
            step(TS(q25[:, 1:2], q25[:, 0:1], float(TILES - 1), None, ALU.add))
            h0, h1 = hit[0:QB, 0, :], hit[0:QB, 1, :]
            step(TS(h0, mmb[0:QB, 0, :], q25[0:QB, 1:2], None, ALU.is_le))
            step(STT(out=h1, in0=mmb[0:QB, 1, :], scalar=q25[0:QB, 0:1], in1=h0, op0=ALU.is_ge, op1=ALU.mult))
            step(STT(out=h0, in0=chunk[0:QB, :], scalar=1.0, in1=h1, op0=ALU.add, op1=ALU.mult))
            step(dve.tensor_reduce(lohi[0:QB, 1:2], h0, AX.X, ALU.max))
            step(STT(out=h0, in0=h1, scalar=-4.0 * NCH, in1=chunk[0:QB, :], op0=ALU.mult, op1=ALU.add))
            step(dve.tensor_reduce(lohi[0:QB, 0:1], h0, AX.X, ALU.min))
            step(TS(lohi[0:QB, 0:1], lohi[0:QB, 0:1], 4.0 * NCH, NCH - 1.0, ALU.add, ALU.min))
            step(TS(lohi[0:QB, 0:1], lohi[0:QB, 0:1], 0.0, None, ALU.max))
            step(TT(lohi[0:QB, 2:3], lohi[0:QB, 1:2], lohi[0:QB, 0:1], ALU.subtract))
            step(TS(lohi[0:QB, 2:3], lohi[0:QB, 2:3], -float(W), 0.0, ALU.add, ALU.max))
            dve.tensor_copy(win_i[0:QB, 0:1], lohi[0:QB, 0:1])
            dve.tensor_copy(win_i[0:QB, 1:2], lohi[0:QB, 2:3]).then_inc(s_win, 1)

            dve.wait_ge(s_x, 16)
            for c in range(TILES):
                step(dve.bn_stats(stat6[0:Q, c % 2, :], x_raw[0:Q, c, :]))
                last = dve.bn_aggr(stats[0:Q, c, :], stat6[0:Q, c % 2, :])
            step(last)
            rsqrt(stats[0:Q, :, 1], EPS, dis[0:Q, :], 1)
            for c in range(TILES):
                last = TS(hd[0:Q, c, :], x_raw[0:Q, c, :], stats[0:Q, c, 0:1], dis[0:Q, c:c + 1], ALU.subtract, ALU.mult)
            step(last)
            step(TS(hd[0:Q, :, :], hd[0:Q, :, :], 0.0, None, ALU.max))

            dve.wait_ge(s_small, 80)
            step(dve.memset(reg[:, HOPS:HOPS + 1], 0.0))
            TS(keep[:, :], reg[:, :], -1.0, 1.0, ALU.mult, ALU.add)
            step(TS(anchor[:, :], reg[:, :], ALPHA, None, ALU.mult))

            def magnitude(ap, of, by):
                step(TS(ap, of, by, None, ALU.mult))
                step(STT(out=ap, in0=ap, scalar=-1.0, in1=ap, op0=ALU.mult, op1=ALU.max))

            magnitude(grow[:, 0, :], reg[:, 0:HOPS], 1.0 - ALPHA)
            magnitude(grow[:, 1, :], keep[:, 0:HOPS], 1.0)
            step(TT(grow[:, 0, :], grow[:, 0, :], grow[:, 1, :], ALU.add))
            magnitude(grow[:, 1, :], anchor[:, 0:HOPS], BOUND)
            step(dve.memset(bnd[:, 0:1], BOUND))
            for h in range(HOPS):
                step(STT(out=bnd[:, h + 1:h + 2], in0=bnd[:, h:h + 1], scalar=grow[:, 0, h:h + 1],
                         in1=grow[:, 1, h:h + 1], op0=ALU.mult, op1=ALU.add))

            def powers(value, exponent, power, inverse):
                step(TS(exponent, value.bitcast(I32), 23, None, ALU.logical_shift_right))
                step(TS(exponent, exponent, -1.0, 268.0, ALU.mult, ALU.add))
                step(TS(exponent, exponent, 1.0, 253.0, ALU.max, ALU.min))
                step(TS(power, exponent, 23, None, ALU.logical_shift_left))
                step(TS(exponent, exponent, -1.0, 254.0, ALU.mult, ALU.add))
                step(TS(inverse, exponent, 23, None, ALU.logical_shift_left))

            powers(bnd[:, :], expo[:, :], scale[:, :], unscale[:, :])
            step(TS(gain[:, :], reg[:, 0:HOPS], (1.0 - ALPHA) * UNIT, None, ALU.mult))
            step(TT(gain[:, :], gain[:, :], unscale[:, 0:HOPS].bitcast(F32), ALU.mult))
            dve.wait_ge(s_raw, 48)
            step(dve.tensor_reduce(mbound[:, 0:4], w_raw[:, 0:4, :], AX.X, ALU.add, apply_absolute_value=True))
            magnitude(bias_nat[:, :], bias_nat[:, :], 1.0)
            step(STT(out=mbound[:, 0:4], in0=mbound[:, 0:4], scalar=BOUND * 1.001, in1=bias_nat[:, :],
                     op0=ALU.mult, op1=ALU.add))
            dve.tensor_reduce(mbound[:, 5:6], mbound[:, 0:4], AX.X, ALU.max).then_inc(s_bnd, 1)
            dve.wait_ge(s_bndr, 1)
            powers(mbound[:, 6:7], mexp[:, 0:1], mscale[:, 0:1].bitcast(I32), mexp[:, 1:2])
            step(TS(mscale[:, 1:2], mexp[:, 1:2].bitcast(F32), UNIT, None, ALU.mult))
            dve.wait_ge(s_wtr, 1)
            TS(wt_msg[:, :], ps[:, 6, :], mscale[:, 0:1], None, ALU.mult)
            TS(bias_msg[:, :], bias_msg[:, :], mscale[:, 0:1], None, ALU.mult)
            dve.tensor_copy(wt_ih[:, :], ps[:, 7, 0:3 * F])
            dve.tensor_copy(wt_hh[:, 0:F], ps[:, 7, 3 * F:4 * F])
            dve.tensor_copy(wt_hh[:, F:3 * F], ps[:, 5, 0:2 * F])
            step(TT(bias_rz[:, :], bias_ih[:, 0:2], bias_hh[:, 0:2], ALU.add))

            for m in (big1, big2):
                last = dve.memset(m[:, :].bitcast(DT.uint16).rearrange("p (n q) -> p n q", q=64)[:, :, 63:64], 0)
            step(last)
            dve.sem_inc(s_prep, 1)
            dve.sem_inc(s_taken, 2)
            dve.sem_inc(s_hot, 2 * W)

            dve.wait_ge(s_win_in, 16)
            made = dve.alloc_register("extras_made")
            dve.reg_mov(made, 0)
            made_g = dve.alloc_register("extras_made_by_type")
            dve.reg_mov(made_g, 0)
            dve.sem_inc(s_more_used, 1)
            dve.sem_inc(s_mfull, 1)
            dve.sem_inc(s_mp, 1)
            dve.sem_inc(s_ct, 1)

            def onehots(n, q, b, m=None):
                many = dve.value_load(windows[0:1, ds(q + MANY, 1)], min_val=0, max_val=NCH)
                dve.wait_ge(s_wst, n + 1)
                if m is not None:
                    weights = win[0:CH, b, 1, :]
                    steps_g(TS(weights, weights, want[0:CH, ds(m, 1)], every[0:CH, ds(m, 1)], ALU.is_equal, ALU.max))
                if not isinstance(n, int):
                    dve.wait_ge(s_hot_used, W * n)
                TT(hot_place[0:CH, b, :, :], iota_place[0:CH, :, :],
                   win_p[0:CH, b:b + 1, :].broadcast_to([CH, 128, W]), ALU.is_equal)
                for w in range(W):
                    dve.wait_ge(s_hot_used, W * n + w + 1)
                    TS(hot_pair[0:CH, w, :], iota_pair[0:CH, :], win[0:CH, b, 0, w:w + 1],
                       win[0:CH, b, 1, w:w + 1], ALU.is_equal, ALU.mult).then_inc(s_hot, 1)
                with dve.If(many > 0):
                    lo = dve.value_load(windows[0:1, ds(q, 1)], min_val=0, max_val=NCH - 1)
                    with dve.Fori(0, many) as j:
                        dve.reg_add(made, made, 1)
                        dve.wait_ge(s_more_used, dve.snap(made))
                        col = nc.s_assert_within(lo + j + W, 0, PAD - 1)
                        TS(win_x[0:CH, 0:1], keys[0:CH, ds(col, 1)], q_off[0:CH, ds(q, 1)], None, ALU.subtract)
                        dve.tensor_copy(win_x[0:CH, 1:3], tab[0:CH, :, ds(col, 1)].rearrange("p j o -> p (j o)"))\
                           .then_inc(s_xs, 1)
                        dve.wait_ge(s_xs, dve.snap(made))
                        if m is not None:
                            TS(win_x[0:CH, 2:3], win_x[0:CH, 2:3], want[0:CH, ds(m, 1)], every[0:CH, ds(m, 1)],
                               ALU.is_equal, ALU.max).then_inc(s_xs_g, 1)
                            dve.reg_add(made_g, made_g, 1)
                            dve.wait_ge(s_xs_g, dve.snap(made_g))
                        TS(hot_place_x[0:CH, :], iota_place[0:CH, :, 0], win_x[0:CH, 1:2], None, ALU.is_equal)
                        TS(hot_pair[0:CH, W, :], iota_pair[0:CH, :], win_x[0:CH, 0:1], win_x[0:CH, 2:3],
                           ALU.is_equal, ALU.mult).then_inc(s_more, 1)

            onehots(0, 0, 0)
            with dve.Fori(0, QB // 2 - 1) as i:
                onehots(2 * i + 1, 2 * i + 1, 1)
                onehots(2 * i + 2, 2 * i + 2, 0)
            onehots(QB - 1, QB - 1, 1)
            dve.wait_ge(s_flagq, QB + 2)
            dve.tensor_reduce(over1[:, 0:1], over[:, :], AX.X, ALU.max).then_inc(s_flag, 1)
            dve.wait_ge(s_flagp, 1)
            TS(flag[0:1, 0:1], ps[0:1, 4, 0:1], 0.0, None, ALU.is_gt).then_inc(s_flagi, 1)

            dve.wait_ge(s_flagi, 1)
            over_any = dve.value_load(flag[0:1, 0:1], min_val=0, max_val=1)

            with dve.If(over_any > 0):
                dve.wait_ge(s_packed, 80)
                for m in range(TYPES + 1):
                    dve.memset(want[:, m:m + 1], ONE + 4.0 ** m)
                    dve.memset(every[:, m:m + 1], float(m == TYPES))
                for d in range(DIGITS):
                    last = dve.memset(mask[:, d:d + 1], 15 << 4 * d)
                steps_g(last)
                dve.sem_inc(s_tables, 1)
                dve.sem_inc(s_epi, 1)
                dve.sem_inc(s_epi_m, 1)

                def wait_carrier():
                    dve.memset(scrap[:, :], 0)

                def digit(n, q, b, d):
                    dve.wait_ge(s_flagq, n + 3)
                    steps_g(TS(cnt_m[:, :], cnt_i[:, b, :], mask[:, ds(d, 1)], None, ALU.bitwise_and))
                    wait_carrier()
                    steps_g(TS(cnt_8[:, :], cnt_m[:, :], 1.0 / UNIT, None, ALU.mult, saturate=False))
                    steps_g(dve.tensor_copy(big1[:, :].rearrange("p (n q) -> p n q", q=128)[:, :, ds(q, 1)]
                                            .rearrange("p n q -> p (n q)"), cnt_8[:, :].bitcast(U8)))
                    dve.sem_inc(s_taken, 1)

                wait_carrier()
                with dve.Fori(0, TYPES + 1) as m:
                    steps_g.loop(m, 8 * DIGITS * (QB // 2))
                    outer = steps_g.base
                    with dve.Fori(0, DIGITS) as d:
                        with dve.Fori(0, QB // 2) as i:
                            steps_g.base, steps_g.k = outer + 8 * (QB // 2) * d + 8 * i, 0
                            for b in range(2):
                                n = QB * (m * DIGITS + d + 1) + 2 * i + b
                                onehots(n, 2 * i + b, b, m)
                                digit(n, 2 * i + b, b, d)
                            assert steps_g.k == 8
                        dve.wait_ge(s_plane, 16 * (m * DIGITS + d + 1))
                    steps_g.k = steps_g.per
                steps_g.done(TYPES + 1)
                with dve.Fori(0, TILES) as c:
                    dve.wait_ge(s_sacc, c + 2)
                    steps_g.loop(c, 1)
                    steps_g(TS(deg[0:Q, ds(c, 1)], ps[0:Q, 0, 0:1], UNIT, 1.0, ALU.mult, ALU.max))
                    dve.sem_inc(s_epi, 1)
                steps_g.done(TILES)
            with dve.If(over_any < 1):
                dve.wait_ge(s_deg, 1)
                TS(deg[0:Q, :], ps[0:Q, 6, 0:TILES], UNIT, 1.0, ALU.mult, ALU.max).then_inc(s_degd, 1)
                dve.wait_ge(s_degd, 1)
            step(dve.reciprocal(inv_deg[0:Q, :], deg[0:Q, :]))
            rsqrt(deg[0:Q, :], 0.0, dis[0:Q, :], 2)
            step(TT(sqd[0:Q, :], deg[0:Q, :], dis[0:Q, :], ALU.mult))
            for c in range(TILES):
                last = TS(hd[0:Q, c, :], hd[0:Q, c, :], dis[0:Q, c:c + 1], None, ALU.mult)
            step(last)

            def split(step, value, c, parts, power, rest=None):
                at = parts[0:Q, c, :, :] if isinstance(c, int) else parts[0:Q, ds(c, 1), :, :].rearrange("p c h f -> p (c h) f")
                step(TS(at[:, 0, :], value, power, None, ALU.mult))
                if rest:
                    rest()
                return STT(out=at[:, 1, :], in0=value, scalar=power, in1=at[:, 0, :], op0=ALU.mult, op1=ALU.subtract)

            def tile_of(m, c):
                return m[0:Q, c, :] if isinstance(c, int) else m[0:Q, ds(c, 1), :].rearrange("p c f -> p (c f)")

            def column(m, c):
                return m[0:Q, c:c + 1] if isinstance(c, int) else m[0:Q, ds(c, 1)]

            def carry(step, value, c, h):
                step(TS(hop_tmp[0:Q, 2, :], value, keep[0:Q, ds(h, 1)], None, ALU.mult))
                step(STT(out=tile_of(g, c), in0=tile_of(hd, c), scalar=anchor[0:Q, ds(h, 1)], in1=hop_tmp[0:Q, 2, :],
                         op0=ALU.mult, op1=ALU.add))

            def hop_tile(step, bank, c, h, parts, read):
                power = scale[0:Q, ds(h + 1, 1)].bitcast(F32)
                new = hop_tmp[0:Q, 1, :]
                step(STT(out=hop_tmp[0:Q, 0, :], in0=bank[:, 0:F], scalar=column(coef, c),
                         in1=tile_of(g, c), op0=ALU.mult, op1=ALU.add))
                step(STT(out=new, in0=bank[:, F:2 * F], scalar=column(coef, c),
                         in1=hop_tmp[0:Q, 0, :], op0=ALU.mult, op1=ALU.add))
                read()
                return split(step, new, c, parts, power, lambda: carry(step, new, c, h + 1))

            dve.sem_inc(s_ring, RING)
            for c in range(TILES):
                split(step, hd[0:Q, c, :], c, parts0, scale[0:Q, 0:1].bitcast(F32)).then_inc(s_parts, 1)
            for c in range(TILES):
                carry(step, hd[0:Q, c, :], c, 0)
            dve.wait_ge(s_packed, 80)
            with dve.If(over_any > 0):
                with dve.Fori(0, HOPS // 2) as i:
                    steps_g.loop(i, 2 * (1 + 6 * TILES))
                    outer = steps_g.base
                    for par, parts in enumerate((parts1, parts0)):
                        steps_g.base, steps_g.k = outer + par * (1 + 6 * TILES), 0
                        steps_g(TS(coef[0:Q, :], inv_deg[0:Q, :], gain[0:Q, ds(2 * i + par, 1)], None, ALU.mult))
                        dve.memset(scrap[:, :], 0)
                        with dve.Fori(0, TILES) as c:
                            steps_g.base, steps_g.k = outer + par * (1 + 6 * TILES) + 1 + 6 * c, 0
                            dve.wait_ge(s_sacc, TILES * (2 * i + par + 1) + c + 2)
                            steps_g(hop_tile(steps_g, ps[0:Q, 0, :], c, 2 * i + par, parts, lambda: None))
                            dve.sem_inc(s_epi, 1)
                            assert steps_g.k == 6
                    steps_g.k = steps_g.per
                steps_g.done(HOPS // 2)
            with dve.If(over_any < 1):
                with dve.Fori(0, HOPS // 2) as i:
                    steps.loop(i, 2 * (1 + 5 * TILES))
                    for par, parts in enumerate((parts1, parts0)):
                        step(TS(coef[0:Q, :], inv_deg[0:Q, :], gain[0:Q, ds(2 * i + par, 1)], None, ALU.mult))
                        for c in range(TILES):
                            n = par * TILES + c
                            dve.wait_ge(s_acc, 2 * TILES * i + n + 1)
                            hop_tile(step, ps[0:Q, n % RING, :], c, 2 * i + par, parts,
                                     lambda: dve.sem_inc(s_ring, 1)).then_inc(s_parts, 1)
                steps.done(HOPS // 2)
            steps = Chain(dve, s_dve_late)

            dve.wait_ge(s_xa, 16)
            for c in range(TILES):
                last = STT(out=x2[0:Q, c, :], in0=g[0:Q, c, :], scalar=sqd[0:Q, c:c + 1], in1=x_again[0:Q, c, :],
                           op0=ALU.mult, op1=ALU.add)
            last.then_inc(s_x2, 1)
            dve.wait_ge(s_x2, 1)
            for c in range(TILES):
                step(dve.bn_stats(stat6[0:Q, c % 2, :], x2[0:Q, c, :]))
                last = dve.bn_aggr(stats[0:Q, c, :], stat6[0:Q, c % 2, :])
            step(last)
            rsqrt(stats[0:Q, :, 1], EPS, dis[0:Q, :], 3)
            for c in range(TILES):
                TS(normed[0:Q, c, :], x2[0:Q, c, :], stats[0:Q, c, 0:1], dis[0:Q, c:c + 1],
                   ALU.subtract, ALU.mult).then_inc(s_nrm, 1)

            dve.sem_inc(s_slot_free, 2)
            dve.wait_ge(s_x2_out, 16)

            def low(s, a):
                dve.wait_ge(s_hi, TILES * s + a + 1)
                TT(m_parts[0:Q, a, 1, :], m_full[0:Q, a % 2, :], m_parts[0:Q, a, 0, :], ALU.subtract).then_inc(s_mp, 1)

            def messages(s):
                for a in range(TILES):
                    dve.wait_ge(s_mp, TILES * s + max(a, 1))
                    dve.wait_ge(s_m, TILES * s + a + 1)
                    TT(m_full[0:Q, a % 2, :], ps[0:Q, 6 + a % 2, :], bias_msg[0:Q, :], ALU.add).then_inc(s_mfull, 1)
                    if a:
                        low(s, a - 1)
                low(s, TILES - 1)

            def update(step, turn, n, e, wide, meanwhile=None):
                dve.wait_ge(s_gn, turn + 1)
                dve.wait_ge(s_sig, 2 * turn + 2)
                step(STT(out=cand_h[:, 0:n], in0=ps[:, 5, 0:n], scalar=bias_hh[:, 2:3], in1=gate_r[:, 0:n],
                         op0=ALU.add, op1=ALU.mult))
                TT(cand_t[:, 0:n], ps[:, 4, 0:n], cand_h[:, 0:n], ALU.add).then_inc(s_ct, 1)
                if meanwhile:
                    meanwhile()
                dve.wait_ge(s_tanh, turn + 1)
                step(TT(wide(diff), e, wide(cand), ALU.subtract))
                dve.wait_ge(s_sig, 2 * turn + 3)
                step(TT(diff[:, 0:n], diff[:, 0:n], gate_z[:, 0:n], ALU.mult))
                step(TT(e, wide(cand), wide(diff), ALU.add))

            with dve.If(over_any > 0):
                steps_g.base, steps_g.k = steps_g.base + steps_g.k, 0
                start = steps_g.base
                with dve.Fori(0, STEPS) as s:
                    messages(s)
                    with dve.Fori(0, TILES) as c:
                        steps_g.base, steps_g.k = start + 4 * (TILES * s + c), 0
                        update(steps_g, TILES * s + c, Q, emb[:, ds(c, 1), :].rearrange("p c q -> p (c q)"),
                               lambda m: m[:, 0:Q])
                        assert steps_g.k == 4
                        dve.sem_inc(s_epi_m, 1)
            with dve.If(over_any < 1):
                for k in range(BLOCKS):
                    dve.wait_ge(s_pblk[k], 16)
                with dve.Fori(0, STEPS) as s:
                    steps.loop(s, 4 * BLOCKS)

                    def unpack(k, t):
                        u = TYPES * (BLOCKS * s + k) + t
                        words = SIZES[k] * TILE_BYTES // 4
                        dve.wait_ge(s_slot_free, u + 1)
                        TS(slots[:, t % 2, 0:words * 4].bitcast(I32),
                           big1[:, START[k] * TILE_BYTES:(START[k] + SIZES[k]) * TILE_BYTES].bitcast(I32),
                           2 * t, LOWBITS, ALU.logical_shift_right, ALU.bitwise_and).then_inc(s_slot, 1)

                    unpack(0, 0)
                    unpack(0, 1)
                    messages(s)
                    unpack(0, 2)
                    unpack(0, 3)
                    for k in range(BLOCKS):
                        more = k + 1 < BLOCKS
                        if more:
                            unpack(k + 1, 0)
                            unpack(k + 1, 1)
                        n = SIZES[k] * Q
                        update(step, BLOCKS * s + k, n, emb[:, START[k]:START[k] + SIZES[k], :],
                               lambda m: m[:, 0:n].rearrange("p (c q) -> p c q", q=Q),
                               (lambda: unpack(k + 1, 2)) if more else None)
                        dve.sem_inc(s_emb, 1)
                        if more:
                            unpack(k + 1, 3)
                steps.done(STEPS)

            dve.wait_ge(s_x2b, 16)
            for k in range(BLOCKS):
                dve.wait_ge(s_otr, k + 1)
                a, z = START[k], START[k] + SIZES[k]
                TT(result[0:Q, a:z, :], ps[0:Q, k, 0:SIZES[k] * F].rearrange("p (c f) -> p c f", f=F),
                   x2_back[0:Q, a:z, :], ALU.add).then_inc(s_res, 1)


_INS = ["x", "src", "dst", "edge_type_4", "L0_gnn_layer_reg", "L1_gnn_W_msg", "L1_gnn_b_msg",
        "L1_gnn_w_ih", "L1_gnn_w_hh", "L1_gnn_b_ih", "L1_gnn_b_hh"]


def kernel(**inputs):
    import numpy as _np
    import concourse.bacc as _bacc
    from concourse import mybir as _mybir
    from concourse.bass_utils import run_bass_kernel_spmd as _run

    nc = _bacc.Bacc("TRN2", target_bir_lowering=False, num_devices=1)
    arrays, args = {}, []
    for name in _INS:
        a = _np.ascontiguousarray(inputs[name])
        arrays[f"in_{name}"] = a
        args.append(nc.dram_tensor(f"in_{name}", a.shape, _mybir.dt.from_np(a.dtype), kind="ExternalInput").ap())
    out = nc.dram_tensor("out_0", (N, F), F32, kind="ExternalOutput").ap()
    build(nc, *args, out)
    r = _run(nc, [arrays], core_ids=[0])
    return r.results[0]["out_0"]
```

```python
from contextlib import ExitStack

import numpy as np
import concourse.bass as bass
from concourse import mybir

DT = mybir.dt
F32, F16, F8, I32, U8 = DT.float32, DT.float16, DT.float8e4, DT.int32, DT.uint8
ALU = mybir.AluOpType
ACT = mybir.ActivationFunctionType
AX = mybir.AxisListType
ds = bass.ds

N = 3125
E = 103125
F = 128
TILES = 25
Q = N // TILES
CH = 125
NCH = E // CH
ROWS = 75
PER = NCH // ROWS
W = 8
QB = Q + 1
PAD = NCH + W + 7
CA = TILES * TILES
TYPES = 4
HOPS = 10
STEPS = 4
ALPHA = 0.1
EPS = 1e-5
ONE = 1024
UNIT = 512.0
BOUND = 11.4
EMB = 2048.0
MAGIC = 12582912.0
SIZES = [4, 4, 4, 4, 3, 3, 3]
START = [sum(SIZES[:k]) for k in range(7)]
BLOCKS = len(SIZES)
BLOCK_OF = [k for k, n in enumerate(SIZES) for _ in range(n)]
AHEAD = 3
LAG = 20
RING = 5
PS0 = 12
DIGITS = 5
LOADS = (TYPES + 1) * DIGITS
BIG = CA * 128
TILE_BYTES = TILES * 128
LO, MANY, LOWBITS = 0, QB, 0x03030303


class Chain:

    def __init__(self, eng, sem):
        self.eng, self.sem, self.base, self.k = eng, sem, 0, 0

    def __call__(self, ins):
        self.k += 1
        ins.then_inc(self.sem, 1)
        self.eng.wait_ge(self.sem, self.base + self.k)

    def loop(self, i, per):
        self.start, self.per = self.base + self.k, per
        self.base, self.k = self.start + i * per, 0

    def done(self, count):
        assert self.k == self.per, (self.k, self.per)
        self.base, self.k = self.start + count * self.per, 0


def build(nc, x, src, dst, edge_type, layer_reg, w_msg, b_msg, w_ih, w_hh, b_ih, b_hh, out):
    scr_mm = nc.dram_tensor("chunk_minmax", (2, NCH), F32).ap()
    scr_win = nc.dram_tensor("windows", (2, QB), I32).ap()
    packed_dram = nc.dram_tensor("packed_counts", (128, BIG), U8).ap()
    x2_dram = nc.dram_tensor("x_after_hops", (Q, TILES * F), F32).ap()
    digits_dram = nc.dram_tensor("digit_counts", (LOADS, 128, BIG), U8).ap()

    ctx = ExitStack()
    with ctx:
        def sb(name, shape, dt, where=None):
            return (where or ctx).enter_context(nc.sbuf_tensor(name, shape, dt))

        def sem(name):
            return ctx.enter_context(nc.semaphore(name))

        big1 = sb("big1", [128, BIG], U8)
        tot = big1[:, :].rearrange("p (c a q) -> p c a q", c=TILES, a=TILES)
        tot_f8 = big1[:, :].bitcast(F8).rearrange("p (c a q) -> p c a q", c=TILES, a=TILES)
        ident = sb("ident", [128, 128], F32)
        w_parts = sb("w_parts", [128, 2, TYPES * F], F16)
        wt_msg = w_parts[:, :, :].bitcast(F32).rearrange("p h m -> p (h m)")
        wt_ih = sb("wt_ih", [128, 3 * F], F32)
        wt_hh = sb("wt_hh", [128, 3 * F], F32)
        bias_msg = sb("bias_msg", [128, TYPES * F], F32)
        bias_ih = sb("bias_ih", [128, 3], F32)
        bias_hh = sb("bias_hh", [128, 3], F32)
        bias_rz = sb("bias_rz", [128, 2], F32)
        bias_nat = sb("bias_nat", [128, TYPES], F32)
        reg = sb("reg", [128, HOPS + 1], F32)
        keep = sb("keep", [128, HOPS + 1], F32)
        anchor = sb("anchor", [128, HOPS + 1], F32)
        grow = sb("grow", [128, 2, HOPS], F32)
        bnd = sb("bnd", [128, HOPS + 1], F32)
        expo = sb("expo", [128, HOPS + 1], I32)
        scale = sb("scale", [128, HOPS + 1], I32)
        unscale = sb("unscale", [128, HOPS + 1], I32)
        gain = sb("gain", [128, HOPS], F32)
        coef = sb("coef", [128, TILES], F32)
        mbound = sb("mbound", [128, 8], F32)
        mexp = sb("mexp", [128, 3], I32)
        mscale = sb("mscale", [128, 2], F32)
        deg = sb("deg", [128, TILES], F32)
        inv_deg = sb("inv_deg", [128, TILES], F32)
        rstd = sb("rstd", [128, TILES], F32)
        dis = sb("dis", [128, TILES], F32)
        to_hd = sb("to_hd", [128, 2, TILES], F32)
        sqd = sb("sqd", [128, TILES], F32)
        stat6 = sb("stat6", [128, 2, 6], F32)
        stats = sb("stats", [128, TILES, 2], F32)
        rs = sb("rs", [128, 4, TILES], F32)
        over = sb("over", [128, QB], F32)
        over1 = sb("over1", [128, 2], F32)
        neg_lim = sb("neg_lim", [128, 1], F32)
        windows = sb("windows_row", [1, 2 * QB], I32)
        flag = sb("flag", [1, 1], I32)
        both0 = sb("both0", [128, 1], F32)
        scrap = sb("scrap", [128, 1], I32)
        ones16 = sb("ones16", [128, 128], F16)
        onesf = sb("onesf", [128, 1], F32)
        hd = sb("hd", [128, TILES, F], F32)

        with ExitStack() as b:
            keys = sb("keys", [128, PAD], F32, b)
            tab = sb("tab", [128, 2, PAD], F16, b)
            win = sb("win", [128, 2, 2, W], F32, b)
            win_p = sb("win_p", [128, 2, W], F16, b)
            win_x = sb("win_x", [128, 3], F32, b)
            hot_pair = sb("hot_pair", [128, W + 1, CA + 1], F16, b)
            hot_place = sb("hot_place", [128, 2, 128, W], F16, b)
            hot_place_x = sb("hot_place_x", [128, 128], F16, b)
            iota_pair = sb("iota_pair", [128, CA + 1], F16, b)
            iota_place = sb("iota_place", [128, 128, W], F16, b)
            q_off = sb("q_off", [128, QB], F32, b)
            sums = sb("sums", [128, CA], DT.uint16, b)
        with ExitStack() as b:
            g = sb("g", [128, TILES, F], F32, b)
            parts0 = sb("parts0", [128, TILES, 2, F], F16, b)
            hop_tmp = sb("hop_tmp", [128, 3, F], F32, b)
        with ExitStack() as b:
            r_t = sb("r_t", [128, 2, 512], F32, b)
            gate_r = sb("gate_r", [128, 512], F32, b)
            gate_z = sb("gate_z", [128, 512], F32, b)
            cand = sb("cand", [128, 512], F32, b)
            emb_parts = sb("emb_parts", [128, 2, TILES, Q], F16, b)
            m_full = sb("m_full", [128, 2, 512], F32, b)
        emb = hd[:, :, 0:Q]

        sb("shared_room", [128, 27 * 1024 + 64], U8)

        with ExitStack() as b:
            big2 = sb("big2", [128, BIG], U8, b)
        packed = big2[:, :].rearrange("p (c a q) -> p c a q", c=TILES, a=TILES)
        with ExitStack() as b:
            edge_i = sb("edge_i", [128, 3, PER * CH], I32, b)
            edge_p = sb("edge_p", [128, 3, PER * CH], F32, b)
            edge_e = sb("edge_e", [128, PER * CH], I32, b)
            stat_x = sb("stat_x", [128, TILES, 6], F32, b)
            edge_t = sb("edge_t", [128, PER * CH], F32, b)
            mm = sb("mm", [128, 2, PER], F32, b)
            mmb = sb("mmb", [128, 2, NCH], F32, b)
            chunk = sb("chunk", [128, NCH], F32, b)
            hit = sb("hit", [128, 2, NCH], F32, b)
            lohi = sb("lohi", [128, 4], F32, b)
            win_i = sb("win_i", [128, 2], I32, b)
            q25 = sb("q25", [128, 2], F32, b)
        with ExitStack() as b:
            parts1 = sb("parts1", [128, TILES, 2, F], F16, b)
            x_again = sb("x_again", [128, TILES, F], F32, b)
            x2 = sb("x2", [128, TILES, F], F32, b)
            normed = sb("normed", [128, TILES, F], F32, b)
        with ExitStack() as b:
            m_parts = sb("m_parts", [128, TILES, 2, TYPES * F], F16, b)
            slots = sb("slots", [128, 2, 4 * TILES * 128], U8, b)
        tile_u8 = big1[:, 0:TYPES * DIGITS * TILE_BYTES].rearrange("p (l n) -> p l n", n=TILE_BYTES)
        tile_f8 = tile_u8.bitcast(F8).rearrange("p l (a q) -> p l a q", q=128)
        with ExitStack() as b:
            cnt_i = sb("cnt_i", [128, 2, CA], I32, b)
            cnt_m = sb("cnt_m", [128, CA], I32, b)
            cnt_8 = sb("cnt_8", [128, CA], F8, b)
            want = sb("want", [128, TYPES + 1], F32, b)
            every = sb("every", [128, TYPES + 1], F32, b)
            mask = sb("mask", [128, DIGITS], I32, b)
        slots_f8 = slots[:, :, :].bitcast(F8).rearrange("p s (c a q) -> p s c a q", c=4, a=TILES)
        x_raw = big1[:, 0:TILES * F * 4].bitcast(F32).rearrange("p (c f) -> p c f", c=TILES)
        w_raw = big1[:, 16384:16384 + 10 * F * 4].bitcast(F32).rearrange("p (t f) -> p t f", t=10)
        x2_back = x_raw
        result = big1[:, 16384:16384 + TILES * F * 4].bitcast(F32).rearrange("p (c f) -> p c f", c=TILES)

        ps = ctx.enter_context(nc.psum_tensor("ps", [128, 8, 512], F32))
        junk = [ps[:, 2 * i + 4:2 * i + 6, :].rearrange("p b n -> p (b n)")[:, PS0:PS0 + CA] for i in range(2)]
        pairs = [ps[:, 2 * i:2 * i + 2, :].rearrange("p b n -> p (b n)")[:, PS0:PS0 + CA] for i in range(2)]

        s_edges = [sem("targets_loaded"), sem("sources_loaded"), sem("types_loaded")]
        s_x, s_raw, s_small = sem("x_loaded"), sem("weights_loaded"), sem("small_loaded")
        s_const = sem("constants_made")
        s_dve, s_dve_late = sem("vector_steps"), sem("late_vector_steps")
        s_mm, s_mm_out, s_mm_in = sem("minmax_made"), sem("minmax_stored"), sem("minmax_loaded")
        s_key, s_tr, s_trc = sem("edge_rows_made"), sem("edge_rows_transposed"), sem("tables_made")
        s_win, s_win_out, s_win_in = sem("windows_made"), sem("windows_stored"), sem("windows_loaded")
        s_wtr, s_wout = sem("weights_transposed"), sem("weights_out")
        s_bnd, s_bndr = sem("message_bound_made"), sem("message_bound_shared")
        s_sq, s_sqr = sem("variance_made"), sem("root_made")
        s_prep = sem("staging_free")
        s_wst, s_hot, s_hot_used = sem("window_staged"), sem("onehots_made"), sem("onehots_used")
        s_xs_g = sem("extra_weighed")
        s_xs, s_more, s_more_used = sem("extra_staged"), sem("extra_made"), sem("extra_used")
        s_taken, s_flagq, s_sums = sem("counts_taken"), sem("excess_noted"), sem("sums_copied_out")
        s_flag, s_flagp, s_flagi = sem("excess_reduced"), sem("excess_summed"), sem("flag_made")
        s_packed = sem("packed_stored")
        s_deg, s_degd = sem("degrees_summed"), sem("degrees_made")
        s_tohd, s_high0 = sem("first_factors_made"), sem("first_high_parts")
        s_parts, s_acc, s_ring = sem("hop_parts_made"), sem("hop_summed"), sem("hop_bank_free")
        s_pblk = [sem(f"packed_loaded{k}") for k in range(BLOCKS)]
        s_xa, s_x2, s_x2_out = sem("x_loaded_again"), sem("x2_made"), sem("x2_stored")
        s_eh, s_el = sem("embedding_high"), sem("embedding_low")
        s_nrm, s_ntr, s_emb = sem("normed_made"), sem("normed_transposed"), sem("embedding_made")
        s_slot, s_slot_free = sem("slot_unpacked"), sem("slot_used")
        s_m, s_mfull, s_hi, s_mp = sem("messages_made"), sem("messages_copied"), sem("high_parts"), sem("message_parts")
        s_rt = sem("messages_summed")
        s_grz, s_gn, s_sig, s_ct, s_tanh = sem("rz_products"), sem("n_products"), sem("rz_gates"), sem("n_sum"), sem("candidate")
        s_tables = sem("general_tables_made")
        s_plane, s_dve_g = sem("digits_stored"), sem("general_vector_steps")
        s_ld, s_sacc, s_epi = sem("tile_loaded"), sem("tile_summed"), sem("tile_finished")
        s_ld_m, s_sacc_m, s_epi_m = sem("typed_tile_loaded"), sem("typed_tile_summed"), sem("embedding_tile_made")
        s_x2b, s_otr, s_res, s_out = sem("x2_back"), sem("embedding_back"), sem("result_made"), sem("out_stored")

        block = ctx.enter_context(nc.Block())

        x_v = x.rearrange("(p t) f -> p (t f)", t=TILES)
        out_v = out.rearrange("(p t) f -> p (t f)", t=TILES)

        @block.sync
        def _(sp):
            for j, a in enumerate((dst, src, edge_type)):
                sp.dma_start(edge_i[0:ROWS, j, :], a.rearrange("(p e) -> p e", p=ROWS)).then_inc(s_edges[j], 16)
            sp.dma_start(x_raw[0:Q, :, :].rearrange("p c f -> p (c f)"), x_v).then_inc(s_x, 16)
            sp.wait_ge(s_mm, 1)
            sp.dma_start(scr_mm.rearrange("s (p k) -> p s k", p=ROWS), mm[0:ROWS, :, :]).then_inc(s_mm_out, 16)
            sp.wait_ge(s_mm_out, 16)
            sp.dma_start(mmb[0:QB, :, :], scr_mm.partition_broadcast(QB)).then_inc(s_mm_in, 16)
            sp.wait_ge(s_win, 1)
            with nc.allow_non_contiguous_dma("126 x 2 words"):
                sp.dma_start(scr_win.rearrange("s q -> q s"), win_i[0:QB, :]).then_inc(s_win_out, 16)
            sp.wait_ge(s_win_out, 16)
            sp.dma_start(windows[0:1, :], scr_win.rearrange("(o s) q -> o (s q)", o=1)).then_inc(s_win_in, 16)
            sp.wait_ge(s_taken, QB + 2)
            for k in range(5):
                sp.dma_start(packed_dram[:, k * BIG // 5:(k + 1) * BIG // 5],
                             big2[:, k * BIG // 5:(k + 1) * BIG // 5]).then_inc(s_packed, 16)
            sp.wait_ge(s_flagi, 1)
            over_any = sp.value_load(flag[0:1, 0:1], min_val=0, max_val=1)
            sp.wait_ge(s_packed, 80)
            sp.dma_start(x_again[0:Q, :, :].rearrange("p c f -> p (c f)"), x_v).then_inc(s_xa, 16)
            with sp.If(over_any < 1):
                for k in range(BLOCKS):
                    sp.wait_ge(s_acc, (HOPS - 1) * TILES + START[k] + SIZES[k])
                    a, z = START[k] * TILE_BYTES, (START[k] + SIZES[k]) * TILE_BYTES
                    sp.dma_start(big1[:, a:z], packed_dram[:, a:z]).then_inc(s_pblk[k], 16)
            sp.wait_ge(s_x2, 1)
            sp.dma_start(x2_dram, x2[0:Q, :, :].rearrange("p c f -> p (c f)")).then_inc(s_x2_out, 16)
            sp.wait_ge(s_x2_out, 16)
            with sp.If(over_any > 0):
                sp.wait_ge(s_sacc_m, TILES * STEPS + 1)
            with sp.If(over_any < 1):
                sp.wait_ge(s_slot, STEPS * BLOCKS * TYPES)
            sp.dma_start(x2_back[0:Q, :, :].rearrange("p c f -> p (c f)"), x2_dram).then_inc(s_x2b, 16)
            for k in range(BLOCKS):
                a, z = START[k] * F, (START[k] + SIZES[k]) * F
                sp.wait_ge(s_res, k + 1)
                sp.dma_start(out_v[:, a:z], result[0:Q, :, :].rearrange("p c f -> p (c f)")[:, a:z]).then_inc(s_out, 16)
            sp.wait_ge(s_out, 16 * BLOCKS)

        @block.gpsimd
        def _(pool):
            pool.memset(ident[:, :], 0.0).then_inc(s_const, 1)
            pool.wait_ge(s_const, 1)
            pool.affine_select(out=ident[:, :], in_=ident[:, :], compare_op=ALU.not_equal, fill=1.0, base=0,
                               pattern=[[-1, 128]], channel_multiplier=1).then_inc(s_const, 1)
            pool.iota(chunk[:, :], [[1, NCH]], base=0, channel_multiplier=0,
                      allow_small_or_imprecise_dtypes=True).then_inc(s_const, 1)
            pool.iota(q25[:, :], [[TILES - 1, 2]], base=0, channel_multiplier=TILES,
                      allow_small_or_imprecise_dtypes=True).then_inc(s_const, 1)
            pool.iota(iota_pair[:, :], [[1, CA + 1]], base=0, channel_multiplier=0,
                      allow_small_or_imprecise_dtypes=True).then_inc(s_const, 1)
            pool.iota(iota_place[:, :, :], [[1, 128], [0, W]], base=0, channel_multiplier=0,
                      allow_small_or_imprecise_dtypes=True).then_inc(s_const, 1)
            pool.iota(q_off[:, :], [[CA, QB]], base=0, channel_multiplier=0,
                      allow_small_or_imprecise_dtypes=True).then_inc(s_const, 1)
            pool.memset(ones16[:, :], 1.0).then_inc(s_const, 1)
            pool.memset(onesf[:, :], 1.0).then_inc(s_const, 1)
            pool.memset(neg_lim[:, :], 0.5 - 4.0 * ONE).then_inc(s_const, 1)
            pool.wait_ge(s_bnd, 1)
            pool.partition_all_reduce(mbound[:, 6:7], mbound[:, 5:6], 128, bass.bass_isa.ReduceOp.max).then_inc(s_bndr, 1)
            pool.wait_ge(s_trc, 3)
            pool.wait_ge(s_win_in, 16)

            def stage(n, q, b):
                lo = pool.value_load(windows[0:1, ds(q, 1)], min_val=0, max_val=NCH)
                pool.wait_ge(s_hot, W * n + W)
                pool.tensor_tensor(win[0:CH, b, 0, :], keys[0:CH, ds(lo, W)], q_off[0:CH, ds(q, 1)].broadcast_to([CH, W]), ALU.subtract)
                pool.tensor_copy(win[0:CH, b, 1, :], tab[0:CH, 1, ds(lo, W)])
                pool.tensor_copy(win_p[0:CH, b, :], tab[0:CH, 0, ds(lo, W)]).then_inc(s_wst, 1)

            with pool.Fori(0, QB // 2) as i:
                stage(2 * i, 2 * i, 0)
                stage(2 * i + 1, 2 * i + 1, 1)
            pool.wait_ge(s_flagi, 1)
            with pool.If(pool.value_load(flag[0:1, 0:1], min_val=0, max_val=1) > 0):
                with pool.Fori(0, LOADS) as load:
                    with pool.Fori(0, QB // 2) as i:
                        for b in range(2):
                            stage(QB * (load + 1) + 2 * i + b, 2 * i + b, b)
                    pool.wait_ge(s_taken, QB * load + 2 * QB + 2)
                    pool.dma_start(digits_dram[ds(load, 1), :, :].rearrange("o p n -> (o p) n"), big1[:, :]).then_inc(s_plane, 16)
                pool.wait_ge(s_plane, 16 * LOADS)
                with pool.Fori(0, HOPS + 1) as u:
                    with pool.Fori(0, TILES) as c:
                        pool.wait_ge(s_sacc, TILES * u + c + 1)
                        for d in range(DIGITS):
                            pool.dma_start(tile_u8[:, d, :], digits_dram[TYPES * DIGITS + d, :, ds(c * TILE_BYTES, TILE_BYTES)])\
                                .then_inc(s_ld, 16)
                pool.wait_ge(s_sacc, TILES * (HOPS + 1) + 1)
                with pool.Fori(0, STEPS) as s:
                    with pool.Fori(0, TILES) as c:
                        pool.wait_ge(s_sacc_m, TILES * s + c + 1)
                        for load in range(TYPES * DIGITS):
                            pool.dma_start(tile_u8[:, load, :], digits_dram[load, :, ds(c * TILE_BYTES, TILE_BYTES)])\
                                .then_inc(s_ld_m, 16)
                pool.wait_ge(s_ld_m, 16 * TYPES * DIGITS * TILES * STEPS)

        @block.scalar
        def _(act):
            act.dma_start(w_raw[:, 0:4, :], w_msg.rearrange("(t j) f -> j t f", t=4)).then_inc(s_raw, 16)
            act.dma_start(w_raw[:, 4:7, :], w_ih.rearrange("(t j) f -> j t f", t=3)).then_inc(s_raw, 16)
            act.dma_start(w_raw[:, 7:10, :], w_hh.rearrange("(t j) f -> j t f", t=3)).then_inc(s_raw, 16)
            act.dma_start(bias_msg[:, :], b_msg.partition_broadcast(128)).then_inc(s_small, 16)
            act.dma_start(reg[:, 0:HOPS], layer_reg.partition_broadcast(128)).then_inc(s_small, 16)
            with nc.allow_non_contiguous_dma("biases by gate"):
                act.dma_start(bias_ih[:, :], b_ih.rearrange("(g p) -> p g", p=128)).then_inc(s_small, 16)
                act.dma_start(bias_hh[:, :], b_hh.rearrange("(g p) -> p g", p=128)).then_inc(s_small, 16)
                act.dma_start(bias_nat[:, :], b_msg.rearrange("(g p) -> p g", p=128)).then_inc(s_small, 16)

            def root(n):
                act.wait_ge(s_sq, n)
                act.activation(rs[0:Q, 1, :], rs[0:Q, 0, :], ACT.Sqrt).then_inc(s_sqr, 1)

            act.wait_ge(s_wtr, 1)
            act.activation(wt_msg, ps[:, 6, :], ACT.Copy)
            act.activation(wt_ih[:, :], ps[:, 7, 0:3 * F], ACT.Copy)
            act.activation(wt_hh[:, 0:F], ps[:, 7, 3 * F:4 * F], ACT.Copy)
            act.activation(wt_hh[:, F:3 * F], ps[:, 5, 0:2 * F], ACT.Copy).then_inc(s_wout, 1)
            act.wait_ge(s_prep, 1)
            act.wait_ge(s_wout, 1)

            act.wait_ge(s_const, 10)
            act.wait_ge(s_win_in, 16)
            act.sem_inc(s_flagq, 2)
            act.sem_inc(s_rt, 1)
            act.sem_inc(s_sig, 1)
            extras = act.alloc_register("extras_expected")
            act.reg_mov(extras, 1)

            def summed(n, q):
                act.wait_ge(s_hot_used, W * n + 2 * W)
                act.reg_add(extras, extras, act.value_load(windows[0:1, ds(q + MANY, 1)], min_val=0, max_val=NCH))
                act.wait_ge(s_more_used, act.snap(extras))
                act.wait_ge(s_flagq, n + 1)

            def evacuate(q, b):
                summed(q, q)
                by_q = [m[:, :].rearrange("p (n q) -> p n q", q=128)[:, :, ds(q, 1)].rearrange("p n q -> p (n q)")
                        for m in (big1, big2)]
                act.activation(by_q[0], pairs[b], ACT.Copy, scale=1.0 / ONE)
                act.wait_ge(s_taken, q + 2)
                act.activation(sums[:, :], pairs[b], ACT.Copy).then_inc(s_sums, 1)
                act.activation(junk[b], pairs[b], ACT.Relu, bias=neg_lim[:, 0:1],
                               accum_out=over[:, ds(q, 1)]).then_inc(s_flagq, 1)
                act.wait_ge(s_sums, q + 1)
                act.activation(by_q[1], sums[:, :].bitcast(U8).rearrange("p (n two) -> p n two", two=2)[:, :, 0],
                               ACT.Copy).then_inc(s_taken, 1)

            with act.Fori(0, QB // 2) as i:
                evacuate(2 * i, 0)
                evacuate(2 * i + 1, 1)
            root(1)
            act.wait_ge(s_flagi, 1)
            over_any = act.value_load(flag[0:1, 0:1], min_val=0, max_val=1)
            with act.If(over_any > 0):
                act.wait_ge(s_tables, 1)
                with act.Fori(0, LOADS) as load:
                    with act.Fori(0, QB // 2) as i:
                        for b in range(2):
                            n = QB * (load + 1) + 2 * i + b
                            summed(n, 2 * i + b)
                            act.wait_ge(s_taken, n + 1)
                            act.activation(cnt_i[:, b, :], pairs[b], ACT.Copy).then_inc(s_flagq, 1)
            root(2)
            act.wait_ge(s_tohd, 1)
            for c in range(TILES):
                act.activation(parts0[0:Q, c, 0, :], hd[0:Q, c, :], ACT.Copy, scale=to_hd[0:Q, 1, c:c + 1]).then_inc(s_high0, 1)
            root(3)
            for k in range(BLOCKS):
                act.wait_ge(s_ntr, k + 1)
                act.activation(emb_parts[:, 0, START[k]:START[k] + SIZES[k], :],
                               ps[:, k, 0:SIZES[k] * Q].rearrange("p (c q) -> p c q", q=Q), ACT.Relu, scale=EMB).then_inc(s_eh, 1)
                act.activation(emb[:, START[k]:START[k] + SIZES[k], :],
                               ps[:, k, 0:SIZES[k] * Q].rearrange("p (c q) -> p c q", q=Q), ACT.Relu).then_inc(s_emb, 1)
            def high(s, first, last):
                for a in range(first, last):
                    act.wait_ge(s_mfull, TILES * s + a + 2)
                    act.activation(m_parts[0:Q, a, 0, :], m_full[0:Q, a % 2, :], ACT.Copy).then_inc(s_hi, 1)

            def emb_high(first, n):
                act.activation(emb_parts[:, 0, ds(first, n), :], emb[:, ds(first, n), :], ACT.Copy, scale=EMB).then_inc(s_eh, 1)

            def update(turn, n, bank, meanwhile=None):
                act.activation(r_t[:, bank, 0:n], ps[:, bank, 0:n], ACT.Copy, scale=mscale[:, 1:2]).then_inc(s_rt, 1)
                if meanwhile:
                    meanwhile()
                act.wait_ge(s_grz, turn + 1)
                act.activation(gate_r[:, 0:n], ps[:, 2, 0:n], ACT.Sigmoid, bias=bias_rz[:, 0:1]).then_inc(s_sig, 1)
                act.activation(gate_z[:, 0:n], ps[:, 3, 0:n], ACT.Sigmoid, bias=bias_rz[:, 1:2]).then_inc(s_sig, 1)
                act.wait_ge(s_ct, turn + 2)
                act.activation(cand[:, 0:n], gate_r[:, 0:n], ACT.Tanh, bias=bias_ih[:, 2:3]).then_inc(s_tanh, 1)

            with act.If(over_any > 0):
                with act.Fori(0, STEPS) as s:
                    high(s, 0, TILES)
                    with act.Fori(0, TILES) as c:
                        act.wait_ge(s_sacc_m, TILES * s + c + 2)
                        update(TILES * s + c, Q, 0)
                        act.wait_ge(s_epi_m, TILES * s + c + 2)
                        emb_high(c, 1)
            with act.If(over_any < 1):
                def next_step():
                    with act.If(s < STEPS - 1):
                        high(s + 1, 0, 2)

                high(0, 0, AHEAD)
                with act.Fori(0, STEPS) as s:
                    high(s, AHEAD, TILES)
                    for k in range(BLOCKS):
                        act.wait_ge(s_slot_free, TYPES * (BLOCKS * s + k + 1) + 2)
                        update(BLOCKS * s + k, SIZES[k] * Q, k % 2, next_step if k == BLOCKS - 1 else None)
                        if k < BLOCKS - 1:
                            act.wait_ge(s_emb, BLOCKS * (s + 1) + k + 1)
                            emb_high(START[k], SIZES[k])
                    with act.If(s < STEPS - 1):
                        high(s + 1, 2, AHEAD)
                        act.wait_ge(s_emb, BLOCKS * (s + 2))
                        emb_high(START[BLOCKS - 1], SIZES[BLOCKS - 1])

        @block.tensor
        def _(pe):
            def wait_alone(sem, value):
                pe.wait_ge(sem, value)
                pe.ldweights(ones16[:, :], tile_position=(0, 0))

            pe.wait_ge(s_const, 2)
            pe.wait_ge(s_raw, 48)
            for t in range(10):
                last = pe.transpose(ps[:, 6 + t // 4 % 2, t % 4 * F:t % 4 * F + F] if t < 8 else
                                    ps[:, 5, (t - 8) * F:(t - 7) * F], w_raw[:, t, :], ident[:, :])
            last.then_inc(s_wtr, 1)
            for j in range(3):
                pe.wait_ge(s_key, j + 1)
                if j == 2:
                    pe.wait_ge(s_trc, 1)
                for k in range(PER):
                    col = k % 6 * ROWS
                    last = pe.transpose(ps[0:CH, j % 2 * 2 + k // 6, col:col + ROWS],
                                        edge_p[0:ROWS, j, k * CH:(k + 1) * CH], ident[0:ROWS, 0:ROWS])
                last.then_inc(s_tr, 1)
            pe.wait_ge(s_trc, 3)
            pe.wait_ge(s_win_in, 16)

            def count(n, q, b):
                first = ps[:, 2 * b, PS0:512]
                second = ps[:, 2 * b + 1, 0:CA - 512 + PS0]
                pe.wait_ge(s_flagq, n + 1)
                for w in range(W):
                    pe.wait_ge(s_hot, W * n + w + 2 * W + 1)
                    pe.matmul(first, hot_place[0:CH, b, :, w], hot_pair[0:CH, w, 0:512 - PS0],
                              start=w == 0, stop=False, skip_group_check=True)
                    last = pe.matmul(second, hot_place[0:CH, b, :, w], hot_pair[0:CH, w, 512 - PS0:CA],
                                     start=w == 0, stop=w == W - 1, skip_group_check=True)
                    last.then_inc(s_hot_used, 1)
                many = pe.value_load(windows[0:1, ds(q + MANY, 1)], min_val=0, max_val=NCH)
                with pe.If(many > 0):
                    with pe.Fori(0, many):
                        pe.reg_add(extras, extras, 1)
                        pe.wait_ge(s_more, pe.snap(extras))
                        pe.matmul(first, hot_place_x[0:CH, :], hot_pair[0:CH, W, 0:512 - PS0],
                                  start=False, stop=False, skip_group_check=True)
                        pe.matmul(second, hot_place_x[0:CH, :], hot_pair[0:CH, W, 512 - PS0:CA],
                                  start=False, stop=False, skip_group_check=True).then_inc(s_more_used, 1)

            extras = pe.alloc_register("extras_seen")
            pe.reg_mov(extras, 0)
            pe.sem_inc(s_hot_used, W)
            with pe.Fori(0, QB // 2) as i:
                count(2 * i, 2 * i, 0)
                count(2 * i + 1, 2 * i + 1, 1)

            pe.wait_ge(s_flag, 1)
            pe.matmul(ps[0:1, 4, 0:1], over1[:, 0:1], onesf[:, 0:1], start=True, stop=True).then_inc(s_flagp, 1)
            pe.wait_ge(s_flagi, 1)
            over_any = pe.value_load(flag[0:1, 0:1], min_val=0, max_val=1)

            def tile_sum(turn, rhs, bank):
                pe.wait_ge(s_epi, turn + 1)
                wait_alone(s_ld, 16 * DIGITS * (turn + 1))
                for d in range(DIGITS):
                    for a in range(TILES):
                        last = pe.matmul(bank, tile_f8[0:Q, d, a, :], rhs(a), start=d == 0 and a == 0,
                                         stop=d == DIGITS - 1 and a == TILES - 1)
                last.then_inc(s_sacc, 1)

            with pe.If(over_any > 0):
                with pe.Fori(0, LOADS) as load:
                    with pe.Fori(0, QB // 2) as i:
                        for b in range(2):
                            count(QB * (load + 1) + 2 * i + b, 2 * i + b, b)
                pe.sem_inc(s_sacc, 1)
                pe.sem_inc(s_sacc_m, 1)
                with pe.Fori(0, TILES) as c:
                    tile_sum(c, lambda a: ones16[0:Q, 0:1], ps[:, 0, 0:1])
            with pe.If(over_any < 1):
                pe.wait_ge(s_taken, QB + 2)
                for c in range(TILES):
                    for a in range(TILES):
                        last = pe.matmul(ps[:, 6, c:c + 1], tot_f8[0:Q, c, a, :], ones16[0:Q, 0:1],
                                         start=a == 0, stop=a == TILES - 1, skip_group_check=True)
                last.then_inc(s_deg, 1)

            def both(parts, a):
                return parts[0:Q, a, :, :].rearrange("p h f -> p (h f)")

            with pe.If(over_any > 0):
                pe.wait_ge(s_parts, TILES)
                with pe.Fori(0, HOPS // 2) as i:
                    for par, parts in enumerate((parts0, parts1)):
                        with pe.Fori(0, TILES) as c:
                            tile_sum(TILES * (2 * i + par + 1) + c, lambda a: both(parts, a), ps[:, 0, 0:2 * F])
            ready = {0: TILES - 3, TILES - 3: TILES - 2, TILES - 2: TILES - 1, TILES - 1: TILES}
            with pe.If(over_any < 1):
                with pe.Fori(0, HOPS // 2) as i:
                    for n in range(2 * TILES):
                        par, c = divmod(n, TILES)
                        wait_alone(s_ring, 2 * TILES * i + n + 1)
                        for a in range(TILES):
                            if c == 0 and a in ready:
                                wait_alone(s_parts, 2 * TILES * i + par * TILES + ready[a])
                            last = pe.matmul(ps[:, n % RING, 0:2 * F], tot_f8[0:Q, c, a, :],
                                             both((parts0, parts1)[par], a), start=a == 0, stop=a == TILES - 1)
                        last.then_inc(s_acc, 1)

            for k in range(BLOCKS):
                pe.wait_ge(s_nrm, START[k] + SIZES[k])
                for j in range(SIZES[k]):
                    last = pe.transpose(ps[:, k, j * Q:(j + 1) * Q], normed[0:Q, START[k] + j, :], ident[0:Q, 0:Q])
                last.then_inc(s_ntr, 1)
            pe.wait_ge(s_emb, BLOCKS)

            def message(s, a):
                pe.wait_ge(s_mfull, TILES * s + max(a, 1))
                for n, (h, w) in enumerate(((0, 0), (0, 1), (1, 0))):
                    last = pe.matmul(ps[0:Q, 6 + a % 2, :], emb_parts[:, h, a, :], w_parts[:, w, :], start=n == 0, stop=n == 2)
                last.then_inc(s_m, 1)

            def gates(turn, n, bank, e):
                r = r_t[:, bank, 0:n]
                pe.wait_ge(s_rt, turn + 2)
                pe.wait_ge(s_sig, 2 * turn + 1)
                pe.wait_ge(s_ct, turn + 1)
                for j in range(2):
                    pe.matmul(ps[:, 2 + j, 0:n], wt_ih[:, j * F:(j + 1) * F], r, start=True, stop=False)
                    last = pe.matmul(ps[:, 2 + j, 0:n], wt_hh[:, j * F:(j + 1) * F], e, start=False, stop=True)
                last.then_inc(s_grz, 1)
                pe.matmul(ps[:, 4, 0:n], wt_ih[:, 2 * F:3 * F], r, start=True, stop=True)
                pe.matmul(ps[:, 5, 0:n], wt_hh[:, 2 * F:3 * F], e, start=True, stop=True).then_inc(s_gn, 1)

            with pe.If(over_any > 0):
                with pe.Fori(0, STEPS) as s:
                    pe.wait_ge(s_el, TILES * s + BLOCKS)
                    for a in range(TILES):
                        message(s, a)
                    wait_alone(s_mp, TILES * s + TILES + 1)
                    with pe.Fori(0, TILES) as c:
                        turn = TILES * s + c
                        pe.wait_ge(s_rt, turn + 1)
                        wait_alone(s_ld_m, 16 * TYPES * DIGITS * (turn + 1))
                        for t in range(TYPES):
                            for d in range(DIGITS):
                                for a in range(TILES):
                                    for h in range(2):
                                        last = pe.matmul(ps[:, 0, 0:Q], m_parts[0:Q, a, h, t * F:(t + 1) * F],
                                                         tile_f8[0:Q, t * DIGITS + d, a, 0:Q],
                                                         start=t == 0 and d == 0 and a == 0 and h == 0,
                                                         stop=t == TYPES - 1 and d == DIGITS - 1 and a == TILES - 1 and h == 1)
                        last.then_inc(s_sacc_m, 1)
                        pe.wait_ge(s_epi_m, turn + 1)
                        gates(turn, Q, 0, emb[:, ds(c, 1), :].rearrange("p c q -> p (c q)"))
                pe.wait_ge(s_epi_m, TILES * STEPS + 1)

            with pe.If(over_any < 1):
                def message_when_ready(s, a):
                    pe.wait_ge(s_el, BLOCKS * s + BLOCK_OF[a] + 1)
                    message(s, a)

                for a in range(AHEAD):
                    message_when_ready(0, a)
                with pe.Fori(0, STEPS) as s:
                    def gather(k, ts, a):
                        for t in ts:
                            for h in range(2):
                                last = pe.matmul(ps[:, k % 2, 0:SIZES[k] * Q], m_parts[0:Q, a, h, t * F:(t + 1) * F],
                                                 slots_f8[0:Q, t % 2, 0:SIZES[k], a, 0:Q],
                                                 start=a == 0 and t == 0 and h == 0,
                                                 stop=a == TILES - 1 and t == TYPES - 1 and h == 1)
                            if a == TILES - 1:
                                last.then_inc(s_slot_free, 1)

                    def block_gates(k):
                        gates(BLOCKS * s + k, SIZES[k] * Q, k % 2, emb[:, START[k]:START[k] + SIZES[k], :])

                    for k in range(BLOCKS):
                        used = TYPES * (BLOCKS * s + k)
                        if k == 0:
                            pe.wait_ge(s_rt, BLOCKS * s + 1)
                            pe.wait_ge(s_slot, used + 2)
                            for a in range(TILES):
                                if a + AHEAD < TILES:
                                    message_when_ready(s, a + AHEAD)
                                wait_alone(s_mp, TILES * s + a + 2)
                                gather(k, (0, 1) if a < LAG else (0,), a)
                            for a in range(LAG, TILES):
                                gather(k, (1,), a)
                            rest = (2, 3)
                        else:
                            pe.wait_ge(s_rt, BLOCKS * s + k)
                            rest = (0, 1, 2, 3)
                        for t in rest:
                            wait_alone(s_slot, used + t + 1)
                            for a in range(TILES):
                                gather(k, (t,), a)
                            if t == 0:
                                block_gates(k - 1)
                    with pe.If(s < STEPS - 1):
                        message_when_ready(s + 1, 0)
                        message_when_ready(s + 1, 1)
                    block_gates(BLOCKS - 1)
                    with pe.If(s < STEPS - 1):
                        message_when_ready(s + 1, 2)
                pe.wait_ge(s_emb, BLOCKS * (STEPS + 1))

            for k in range(BLOCKS):
                for j in range(SIZES[k]):
                    last = pe.transpose(ps[0:Q, k, j * F:(j + 1) * F], emb[:, START[k] + j, :], ident[:, :])
                last.then_inc(s_otr, 1)

        @block.vector
        def _(dve):
            steps, steps_g = Chain(dve, s_dve), Chain(dve, s_dve_g)

            def step(ins):
                steps(ins)

            TS, STT, TT = dve.tensor_scalar, dve.scalar_tensor_tensor, dve.tensor_tensor

            def rsqrt(value, plus, to, n):
                TS(rs[0:Q, 0, :], value, plus, None, ALU.add).then_inc(s_sq, 1)
                dve.wait_ge(s_sqr, n)
                step(dve.reciprocal(rs[0:Q, 2, :], rs[0:Q, 1, :]))
                step(TT(rs[0:Q, 3, :], rs[0:Q, 2, :], rs[0:Q, 2, :], ALU.mult))
                step(TT(rs[0:Q, 3, :], rs[0:Q, 3, :], rs[0:Q, 0, :], ALU.mult))
                step(TS(rs[0:Q, 3, :], rs[0:Q, 3, :], -0.5, 1.5, ALU.mult, ALU.add))
                step(TT(to, rs[0:Q, 3, :], rs[0:Q, 2, :], ALU.mult))

            def magnitude(ap, of, by):
                step(TS(ap, of, by, None, ALU.mult))
                step(STT(out=ap, in0=ap, scalar=-1.0, in1=ap, op0=ALU.mult, op1=ALU.max))

            dve.memset(keys[:, :], -1e6)
            step(dve.memset(tab[:, :, :], 0.0))
            target, source, kind = (edge_i[0:ROWS, j, :] for j in range(3))
            key, place, weight = (edge_p[0:ROWS, j, :] for j in range(3))
            by_chunk = target.rearrange("p (k e) -> p k e", k=PER)
            dve.wait_ge(s_edges[0], 16)
            dve.tensor_reduce(mm[0:ROWS, 0, :], by_chunk, AX.X, ALU.min)
            dve.tensor_reduce(mm[0:ROWS, 1, :], by_chunk, AX.X, ALU.max).then_inc(s_mm, 1)
            tmp = edge_t[0:ROWS, :]
            dve.wait_ge(s_edges[1], 16)
            step(TS(place, source, -float(TILES // 2), 1.0 / TILES, ALU.add, ALU.mult))
            step(TS(place, place, MAGIC, -MAGIC, ALU.add, ALU.add))
            step(STT(out=tmp, in0=place, scalar=-float(TILES), in1=source, op0=ALU.mult, op1=ALU.add))
            STT(out=key, in0=target, scalar=float(TILES), in1=tmp, op0=ALU.mult, op1=ALU.add).then_inc(s_key, 2)
            power = edge_e[0:ROWS, :]
            dve.wait_ge(s_edges[2], 16)
            step(TS(power, kind, 2.0, 127.0, ALU.mult, ALU.add))
            step(TS(power, power, 23, None, ALU.logical_shift_left))
            TS(weight, power.bitcast(F32), float(ONE), None, ALU.add).then_inc(s_key, 1)
            for j in range(3):
                dve.wait_ge(s_tr, j + 1)
                to = (keys[0:CH, :], tab[0:CH, 0, :], tab[0:CH, 1, :])[j][:, 0:NCH].rearrange("e (p k) -> e k p", k=PER)
                for half, (lo, hi) in enumerate(((0, 6), (6, PER))):
                    last = dve.tensor_copy(to[:, lo:hi, :], ps[0:CH, j % 2 * 2 + half, 0:(hi - lo) * ROWS]
                                           .rearrange("e (k p) -> e k p", p=ROWS))
                last.then_inc(s_trc, 1)
            dve.wait_ge(s_mm_in, 16)
            dve.wait_ge(s_const, 10)
            step(TS(q25[:, 1:2], q25[:, 0:1], float(TILES - 1), None, ALU.add))
            h0, h1 = hit[0:QB, 0, :], hit[0:QB, 1, :]
            step(TS(h0, mmb[0:QB, 0, :], q25[0:QB, 1:2], None, ALU.is_le))
            step(STT(out=h1, in0=mmb[0:QB, 1, :], scalar=q25[0:QB, 0:1], in1=h0, op0=ALU.is_ge, op1=ALU.mult))
            step(STT(out=h0, in0=chunk[0:QB, :], scalar=1.0, in1=h1, op0=ALU.add, op1=ALU.mult))
            step(dve.tensor_reduce(lohi[0:QB, 1:2], h0, AX.X, ALU.max))
            step(STT(out=h0, in0=h1, scalar=-4.0 * NCH, in1=chunk[0:QB, :], op0=ALU.mult, op1=ALU.add))
            step(dve.tensor_reduce(lohi[0:QB, 0:1], h0, AX.X, ALU.min))
            step(TS(lohi[0:QB, 0:1], lohi[0:QB, 0:1], 4.0 * NCH, NCH - 1.0, ALU.add, ALU.min))
            step(TS(lohi[0:QB, 0:1], lohi[0:QB, 0:1], 0.0, None, ALU.max))
            step(TT(lohi[0:QB, 2:3], lohi[0:QB, 1:2], lohi[0:QB, 0:1], ALU.subtract))
            step(TS(lohi[0:QB, 2:3], lohi[0:QB, 2:3], -float(W), 0.0, ALU.add, ALU.max))
            dve.tensor_copy(win_i[0:QB, 0:1], lohi[0:QB, 0:1])
            dve.tensor_copy(win_i[0:QB, 1:2], lohi[0:QB, 2:3]).then_inc(s_win, 1)

            dve.wait_ge(s_x, 16)
            for c in range(TILES):
                last = dve.bn_stats(stat_x[0:Q, c, :], x_raw[0:Q, c, :])
            step(last)
            for c in range(TILES):
                last = dve.bn_aggr(stats[0:Q, c, :], stat_x[0:Q, c, :])
            step(last)
            for c in range(TILES):
                last = TS(hd[0:Q, c, :], x_raw[0:Q, c, :], stats[0:Q, c, 0:1], 0.0, ALU.subtract, ALU.max)
            step(last)
            dve.wait_ge(s_small, 80)
            dve.wait_ge(s_raw, 48)
            step(dve.tensor_reduce(mbound[:, 0:4], w_raw[:, 0:4, :], AX.X, ALU.add, apply_absolute_value=True))
            magnitude(bias_nat[:, :], bias_nat[:, :], 1.0)
            step(STT(out=mbound[:, 0:4], in0=mbound[:, 0:4], scalar=BOUND * 1.001, in1=bias_nat[:, :],
                     op0=ALU.mult, op1=ALU.add))
            dve.tensor_reduce(mbound[:, 5:6], mbound[:, 0:4], AX.X, ALU.max).then_inc(s_bnd, 1)
            dve.wait_ge(s_wtr, 1)

            for m in (big1, big2):
                last = dve.memset(m[:, :].bitcast(DT.uint16).rearrange("p (n q) -> p n q", q=64)[:, :, 63:64], 0)
            step(last)
            dve.sem_inc(s_prep, 1)
            dve.sem_inc(s_taken, 2)
            dve.sem_inc(s_hot, 2 * W)

            dve.wait_ge(s_win_in, 16)
            made = dve.alloc_register("extras_made")
            dve.reg_mov(made, 0)
            made_g = dve.alloc_register("extras_made_by_type")
            dve.reg_mov(made_g, 0)
            dve.sem_inc(s_more_used, 1)
            dve.sem_inc(s_mfull, 1)
            dve.sem_inc(s_mp, 1)
            dve.sem_inc(s_ct, 1)

            def onehots(n, q, b, m=None):
                many = dve.value_load(windows[0:1, ds(q + MANY, 1)], min_val=0, max_val=NCH)
                dve.wait_ge(s_wst, n + 1)
                if m is not None:
                    weights = win[0:CH, b, 1, :]
                    steps_g(TS(weights, weights, want[0:CH, ds(m, 1)], every[0:CH, ds(m, 1)], ALU.is_equal, ALU.max))
                if not isinstance(n, int):
                    dve.wait_ge(s_hot_used, W * n)
                TT(hot_place[0:CH, b, :, :], iota_place[0:CH, :, :],
                   win_p[0:CH, b:b + 1, :].broadcast_to([CH, 128, W]), ALU.is_equal)
                for w in range(W):
                    dve.wait_ge(s_hot_used, W * n + w + 1)
                    TS(hot_pair[0:CH, w, :], iota_pair[0:CH, :], win[0:CH, b, 0, w:w + 1],
                       win[0:CH, b, 1, w:w + 1], ALU.is_equal, ALU.mult).then_inc(s_hot, 1)
                with dve.If(many > 0):
                    lo = dve.value_load(windows[0:1, ds(q, 1)], min_val=0, max_val=NCH - 1)
                    with dve.Fori(0, many) as j:
                        dve.reg_add(made, made, 1)
                        dve.wait_ge(s_more_used, dve.snap(made))
                        col = nc.s_assert_within(lo + j + W, 0, PAD - 1)
                        TS(win_x[0:CH, 0:1], keys[0:CH, ds(col, 1)], q_off[0:CH, ds(q, 1)], None, ALU.subtract)
                        dve.tensor_copy(win_x[0:CH, 1:3], tab[0:CH, :, ds(col, 1)].rearrange("p j o -> p (j o)"))\
                           .then_inc(s_xs, 1)
                        dve.wait_ge(s_xs, dve.snap(made))
                        if m is not None:
                            TS(win_x[0:CH, 2:3], win_x[0:CH, 2:3], want[0:CH, ds(m, 1)], every[0:CH, ds(m, 1)],
                               ALU.is_equal, ALU.max).then_inc(s_xs_g, 1)
                            dve.reg_add(made_g, made_g, 1)
                            dve.wait_ge(s_xs_g, dve.snap(made_g))
                        TS(hot_place_x[0:CH, :], iota_place[0:CH, :, 0], win_x[0:CH, 1:2], None, ALU.is_equal)
                        TS(hot_pair[0:CH, W, :], iota_pair[0:CH, :], win_x[0:CH, 0:1], win_x[0:CH, 2:3],
                           ALU.is_equal, ALU.mult).then_inc(s_more, 1)

            onehots(0, 0, 0)
            with dve.Fori(0, QB // 2 - 1) as i:
                onehots(2 * i + 1, 2 * i + 1, 1)
                onehots(2 * i + 2, 2 * i + 2, 0)
            onehots(QB - 1, QB - 1, 1)
            dve.wait_ge(s_wout, 1)
            dve.wait_ge(s_flagq, QB + 2)
            dve.tensor_reduce(over1[:, 0:1], over[:, :], AX.X, ALU.max).then_inc(s_flag, 1)
            dve.wait_ge(s_flagp, 1)
            TS(flag[0:1, 0:1], ps[0:1, 4, 0:1], 0.0, None, ALU.is_gt).then_inc(s_flagi, 1)

            dve.wait_ge(s_flagi, 1)
            over_any = dve.value_load(flag[0:1, 0:1], min_val=0, max_val=1)

            rsqrt(stats[0:Q, :, 1], EPS, rstd[0:Q, :], 1)
            step(dve.memset(reg[:, HOPS:HOPS + 1], 0.0))
            TS(keep[:, :], reg[:, :], -1.0, 1.0, ALU.mult, ALU.add)
            step(TS(anchor[:, :], reg[:, :], ALPHA, None, ALU.mult))

            magnitude(grow[:, 0, :], reg[:, 0:HOPS], 1.0 - ALPHA)
            magnitude(grow[:, 1, :], keep[:, 0:HOPS], 1.0)
            step(TT(grow[:, 0, :], grow[:, 0, :], grow[:, 1, :], ALU.add))
            magnitude(grow[:, 1, :], anchor[:, 0:HOPS], BOUND)
            step(dve.memset(bnd[:, 0:1], BOUND))
            for h in range(HOPS):
                step(STT(out=bnd[:, h + 1:h + 2], in0=bnd[:, h:h + 1], scalar=grow[:, 0, h:h + 1],
                         in1=grow[:, 1, h:h + 1], op0=ALU.mult, op1=ALU.add))

            def powers(value, exponent, power, inverse):
                step(TS(exponent, value.bitcast(I32), 23, None, ALU.logical_shift_right))
                step(TS(exponent, exponent, -1.0, 268.0, ALU.mult, ALU.add))
                step(TS(exponent, exponent, 1.0, 253.0, ALU.max, ALU.min))
                step(TS(power, exponent, 23, None, ALU.logical_shift_left))
                step(TS(exponent, exponent, -1.0, 254.0, ALU.mult, ALU.add))
                step(TS(inverse, exponent, 23, None, ALU.logical_shift_left))

            powers(bnd[:, :], expo[:, :], scale[:, :], unscale[:, :])
            step(TS(gain[:, :], reg[:, 0:HOPS], (1.0 - ALPHA) * UNIT, None, ALU.mult))
            step(TT(gain[:, :], gain[:, :], unscale[:, 0:HOPS].bitcast(F32), ALU.mult))
            dve.wait_ge(s_bndr, 1)
            powers(mbound[:, 6:7], mexp[:, 0:1], mscale[:, 0:1].bitcast(I32), mexp[:, 1:2])
            step(TS(mscale[:, 1:2], mexp[:, 1:2].bitcast(F32), UNIT, None, ALU.mult))
            step(TS(ps[:, 7, :], wt_msg, mscale[:, 0:1], None, ALU.mult))
            step(dve.tensor_copy(w_parts[:, 0, :], ps[:, 7, :]))
            TT(w_parts[:, 1, :], ps[:, 7, :], w_parts[:, 0, :], ALU.subtract)
            TS(bias_msg[:, :], bias_msg[:, :], mscale[:, 0:1], None, ALU.mult)
            step(TT(bias_rz[:, :], bias_ih[:, 0:2], bias_hh[:, 0:2], ALU.add))

            with dve.If(over_any > 0):
                dve.wait_ge(s_packed, 80)
                for m in range(TYPES + 1):
                    dve.memset(want[:, m:m + 1], ONE + 4.0 ** m)
                    dve.memset(every[:, m:m + 1], float(m == TYPES))
                for d in range(DIGITS):
                    last = dve.memset(mask[:, d:d + 1], 15 << 4 * d)
                steps_g(last)
                dve.sem_inc(s_tables, 1)
                dve.sem_inc(s_epi, 1)
                dve.sem_inc(s_epi_m, 1)

                def wait_carrier():
                    dve.memset(scrap[:, :], 0)

                def digit(n, q, b, d):
                    dve.wait_ge(s_flagq, n + 3)
                    steps_g(TS(cnt_m[:, :], cnt_i[:, b, :], mask[:, ds(d, 1)], None, ALU.bitwise_and))
                    wait_carrier()
                    steps_g(TS(cnt_8[:, :], cnt_m[:, :], 1.0 / UNIT, None, ALU.mult, saturate=False))
                    steps_g(dve.tensor_copy(big1[:, :].rearrange("p (n q) -> p n q", q=128)[:, :, ds(q, 1)]
                                            .rearrange("p n q -> p (n q)"), cnt_8[:, :].bitcast(U8)))
                    dve.sem_inc(s_taken, 1)

                wait_carrier()
                with dve.Fori(0, TYPES + 1) as m:
                    steps_g.loop(m, 8 * DIGITS * (QB // 2))
                    outer = steps_g.base
                    with dve.Fori(0, DIGITS) as d:
                        with dve.Fori(0, QB // 2) as i:
                            steps_g.base, steps_g.k = outer + 8 * (QB // 2) * d + 8 * i, 0
                            for b in range(2):
                                n = QB * (m * DIGITS + d + 1) + 2 * i + b
                                onehots(n, 2 * i + b, b, m)
                                digit(n, 2 * i + b, b, d)
                            assert steps_g.k == 8
                        dve.wait_ge(s_plane, 16 * (m * DIGITS + d + 1))
                    steps_g.k = steps_g.per
                steps_g.done(TYPES + 1)
                with dve.Fori(0, TILES) as c:
                    dve.wait_ge(s_sacc, c + 2)
                    steps_g.loop(c, 1)
                    steps_g(TS(deg[0:Q, ds(c, 1)], ps[0:Q, 0, 0:1], UNIT, 1.0, ALU.mult, ALU.max))
                    dve.sem_inc(s_epi, 1)
                steps_g.done(TILES)
            with dve.If(over_any < 1):
                dve.wait_ge(s_deg, 1)
                TS(deg[0:Q, :], ps[0:Q, 6, 0:TILES], UNIT, 1.0, ALU.mult, ALU.max).then_inc(s_degd, 1)
                dve.wait_ge(s_degd, 1)
            step(dve.reciprocal(inv_deg[0:Q, :], deg[0:Q, :]))
            rsqrt(deg[0:Q, :], 0.0, dis[0:Q, :], 2)
            step(TT(to_hd[0:Q, 0, :], rstd[0:Q, :], dis[0:Q, :], ALU.mult))
            step(TS(to_hd[0:Q, 1, :], to_hd[0:Q, 0, :], scale[0:Q, 0:1].bitcast(F32), None, ALU.mult))
            dve.sem_inc(s_tohd, 1)
            def split(step, value, c, parts, power, rest=None):
                at = parts[0:Q, c, :, :] if isinstance(c, int) else parts[0:Q, ds(c, 1), :, :].rearrange("p c h f -> p (c h) f")
                step(TS(at[:, 0, :], value, power, None, ALU.mult))
                if rest:
                    rest()
                return STT(out=at[:, 1, :], in0=value, scalar=power, in1=at[:, 0, :], op0=ALU.mult, op1=ALU.subtract)

            def tile_of(m, c):
                return m[0:Q, c, :] if isinstance(c, int) else m[0:Q, ds(c, 1), :].rearrange("p c f -> p (c f)")

            def column(m, c):
                return m[0:Q, c:c + 1] if isinstance(c, int) else m[0:Q, ds(c, 1)]

            def carry(step, value, c, h):
                step(TS(hop_tmp[0:Q, 2, :], value, keep[0:Q, ds(h, 1)], None, ALU.mult))
                step(STT(out=tile_of(g, c), in0=tile_of(hd, c), scalar=anchor[0:Q, ds(h, 1)], in1=hop_tmp[0:Q, 2, :],
                         op0=ALU.mult, op1=ALU.add))

            def new_features(step, bank, c):
                step(STT(out=hop_tmp[0:Q, 0, :], in0=bank[:, 0:F], scalar=column(coef, c),
                         in1=tile_of(g, c), op0=ALU.mult, op1=ALU.add))
                step(STT(out=hop_tmp[0:Q, 1, :], in0=bank[:, F:2 * F], scalar=column(coef, c),
                         in1=hop_tmp[0:Q, 0, :], op0=ALU.mult, op1=ALU.add))

            def hop_tile(step, bank, c, h, parts, read):
                new = hop_tmp[0:Q, 1, :]
                new_features(step, bank, c)
                read()
                return split(step, new, c, parts, scale[0:Q, ds(h + 1, 1)].bitcast(F32),
                             lambda: carry(step, new, c, h + 1))

            def finish_tile(step, value, c):
                step(STT(out=x2[0:Q, c, :], in0=value, scalar=sqd[0:Q, c:c + 1], in1=x_again[0:Q, c, :],
                         op0=ALU.mult, op1=ALU.add))
                step(dve.bn_stats(stat6[0:Q, c % 2, :], x2[0:Q, c, :]))
                step(dve.bn_aggr(stats[0:Q, c, :], stat6[0:Q, c % 2, :]))

            def unpack(s, k, t):
                u = TYPES * (BLOCKS * s + k) + t
                words = SIZES[k % BLOCKS] * TILE_BYTES // 4
                first = START[k % BLOCKS] * TILE_BYTES
                dve.wait_ge(s_slot_free, u + 1)
                if isinstance(s, int):
                    dve.wait_ge(s_pblk[k], 16)
                TS(slots[:, t % 2, 0:words * 4].bitcast(I32), big1[:, first:first + words * 4].bitcast(I32),
                   2 * t, LOWBITS, ALU.logical_shift_right, ALU.bitwise_and).then_inc(s_slot, 1)

            dve.sem_inc(s_slot_free, 2)
            dve.sem_inc(s_ring, RING)
            for c in range(TILES):
                dve.wait_ge(s_high0, c + 1)
                STT(out=parts0[0:Q, c, 1, :], in0=hd[0:Q, c, :], scalar=to_hd[0:Q, 1, c:c + 1], in1=parts0[0:Q, c, 0, :],
                    op0=ALU.mult, op1=ALU.subtract).then_inc(s_parts, 1)
            dve.wait_ge(s_parts, TILES)
            step(TT(hd[0:Q, :, :], hd[0:Q, :, :], to_hd[0:Q, 0, :].rearrange("p (c o) -> p c o", o=1).broadcast_to([Q, TILES, F]),
                    ALU.mult))
            step(TT(both0[0:Q, :], keep[0:Q, 0:1], anchor[0:Q, 0:1], ALU.add))
            step(TS(g[0:Q, :, :], hd[0:Q, :, :], both0[0:Q, 0:1], None, ALU.mult))
            step(TT(sqd[0:Q, :], deg[0:Q, :], dis[0:Q, :], ALU.mult))
            dve.wait_ge(s_packed, 80)
            with dve.If(over_any > 0):
                with dve.Fori(0, HOPS // 2) as i:
                    steps_g.loop(i, 2 * (1 + 6 * TILES))
                    outer = steps_g.base
                    for par, parts in enumerate((parts1, parts0)):
                        steps_g.base, steps_g.k = outer + par * (1 + 6 * TILES), 0
                        steps_g(TS(coef[0:Q, :], inv_deg[0:Q, :], gain[0:Q, ds(2 * i + par, 1)], None, ALU.mult))
                        dve.memset(scrap[:, :], 0)
                        with dve.Fori(0, TILES) as c:
                            steps_g.base, steps_g.k = outer + par * (1 + 6 * TILES) + 1 + 6 * c, 0
                            dve.wait_ge(s_sacc, TILES * (2 * i + par + 1) + c + 2)
                            steps_g(hop_tile(steps_g, ps[0:Q, 0, :], c, 2 * i + par, parts, lambda: None))
                            dve.sem_inc(s_epi, 1)
                            assert steps_g.k == 6
                    steps_g.k = steps_g.per
                steps_g.done(HOPS // 2)
                dve.wait_ge(s_xa, 16)
                for c in range(TILES):
                    finish_tile(steps_g, g[0:Q, c, :], c)
            with dve.If(over_any < 1):
                def hop(h, par, before):
                    step(TS(coef[0:Q, :], inv_deg[0:Q, :], gain[0:Q, ds(h, 1)], None, ALU.mult))
                    for c in range(TILES):
                        dve.wait_ge(s_acc, before + c + 1)
                        hop_tile(step, ps[0:Q, (par * TILES + c) % RING, :], c, h, (parts1, parts0)[par],
                                 lambda: dve.sem_inc(s_ring, 1)).then_inc(s_parts, 1)

                with dve.Fori(0, HOPS // 2 - 1) as i:
                    steps.loop(i, 2 * (1 + 5 * TILES))
                    for par in range(2):
                        hop(2 * i + par, par, TILES * (2 * i + par))
                steps.done(HOPS // 2 - 1)
                hop(HOPS - 2, 0, TILES * (HOPS - 2))
                step(TS(coef[0:Q, :], inv_deg[0:Q, :], gain[0:Q, HOPS - 1:HOPS], None, ALU.mult))
                dve.wait_ge(s_xa, 16)
                for c in range(TILES):
                    dve.wait_ge(s_acc, TILES * (HOPS - 1) + c + 1)
                    new_features(step, ps[0:Q, (TILES + c) % RING, :], c)
                    dve.sem_inc(s_ring, 1)
                    finish_tile(step, hop_tmp[0:Q, 1, :], c)
                    if c == 17:
                        unpack(0, 0, 0)
                        unpack(0, 0, 1)
            dve.sem_inc(s_x2, 1)
            steps = Chain(dve, s_dve_late)

            rsqrt(stats[0:Q, :, 1], EPS, dis[0:Q, :], 3)
            for c in range(TILES):
                TS(normed[0:Q, c, :], x2[0:Q, c, :], stats[0:Q, c, 0:1], dis[0:Q, c:c + 1],
                   ALU.subtract, ALU.mult).then_inc(s_nrm, 1)

            dve.wait_ge(s_x2_out, 16)

            def low(s, a):
                dve.wait_ge(s_hi, TILES * s + a + 1)
                TT(m_parts[0:Q, a, 1, :], m_full[0:Q, a % 2, :], m_parts[0:Q, a, 0, :], ALU.subtract).then_inc(s_mp, 1)

            def bias(s, a):
                dve.wait_ge(s_mp, TILES * s + max(a, 1))
                dve.wait_ge(s_m, TILES * s + a + 1)
                STT(out=m_full[0:Q, a % 2, :], in0=ps[0:Q, 6 + a % 2, :], scalar=1.0 / EMB, in1=bias_msg[0:Q, :],
                    op0=ALU.mult, op1=ALU.add).then_inc(s_mfull, 1)

            def messages(s, first, last):
                for a in range(first, last):
                    bias(s, a)
                    if a > first:
                        low(s, a - 1)
                low(s, last - 1)

            def update(step, turn, n, e, wide, meanwhile=None):
                dve.wait_ge(s_gn, turn + 1)
                dve.wait_ge(s_sig, 2 * turn + 2)
                step(STT(out=gate_r[:, 0:n], in0=ps[:, 5, 0:n], scalar=bias_hh[:, 2:3], in1=gate_r[:, 0:n],
                         op0=ALU.add, op1=ALU.mult))
                TT(gate_r[:, 0:n], ps[:, 4, 0:n], gate_r[:, 0:n], ALU.add).then_inc(s_ct, 1)
                if meanwhile:
                    meanwhile()
                dve.wait_ge(s_tanh, turn + 1)
                step(TT(wide(gate_r), e, wide(cand), ALU.subtract))
                dve.wait_ge(s_sig, 2 * turn + 3)
                step(TT(gate_r[:, 0:n], gate_r[:, 0:n], gate_z[:, 0:n], ALU.mult))
                step(TT(e, wide(cand), wide(gate_r), ALU.add))

            def emb_low(first, n):
                STT(out=emb_parts[:, 1, ds(first, n), :], in0=emb[:, ds(first, n), :], scalar=EMB,
                    in1=emb_parts[:, 0, ds(first, n), :], op0=ALU.mult, op1=ALU.subtract).then_inc(s_el, 1)

            for k in range(BLOCKS):
                dve.wait_ge(s_emb, k + 1)
                emb_low(START[k], SIZES[k])

            with dve.If(over_any > 0):
                steps_g.base, steps_g.k = steps_g.base + steps_g.k, 0
                start = steps_g.base
                with dve.Fori(0, STEPS) as s:
                    messages(s, 0, TILES)
                    with dve.Fori(0, TILES) as c:
                        steps_g.base, steps_g.k = start + 4 * (TILES * s + c), 0
                        update(steps_g, TILES * s + c, Q, emb[:, ds(c, 1), :].rearrange("p c q -> p (c q)"),
                               lambda m: m[:, 0:Q])
                        assert steps_g.k == 4
                        dve.sem_inc(s_epi_m, 1)
                        dve.wait_ge(s_eh, BLOCKS + TILES * s + c + 1)
                        emb_low(c, 1)
            with dve.If(over_any < 1):
                for k in range(BLOCKS):
                    dve.wait_ge(s_pblk[k], 16)
                messages(0, 0, AHEAD)
                with dve.Fori(0, STEPS) as s:
                    steps.loop(s, 4 * BLOCKS)
                    messages(s, AHEAD, TILES)
                    unpack(s, 0, 2)
                    unpack(s, 0, 3)
                    for k in range(BLOCKS):
                        more = k + 1 < BLOCKS
                        if more:
                            unpack(s, k + 1, 0)
                            unpack(s, k + 1, 1)
                        else:
                            with dve.If(s < STEPS - 1):
                                unpack(s, BLOCKS, 0)
                                unpack(s, BLOCKS, 1)
                                messages(s + 1, 0, 2)
                        n = SIZES[k] * Q
                        update(step, BLOCKS * s + k, n, emb[:, START[k]:START[k] + SIZES[k], :],
                               lambda m: m[:, 0:n].rearrange("p (c q) -> p c q", q=Q),
                               (lambda: unpack(s, k + 1, 2)) if more else None)
                        dve.sem_inc(s_emb, 1)
                        if more:
                            unpack(s, k + 1, 3)
                            dve.wait_ge(s_eh, BLOCKS * (s + 1) + k + 1)
                            emb_low(START[k], SIZES[k])
                    with dve.If(s < STEPS - 1):
                        messages(s + 1, 2, AHEAD)
                        dve.wait_ge(s_eh, BLOCKS * (s + 2))
                        emb_low(START[BLOCKS - 1], SIZES[BLOCKS - 1])
                steps.done(STEPS)

            dve.wait_ge(s_x2b, 16)
            for k in range(BLOCKS):
                dve.wait_ge(s_otr, k + 1)
                a, z = START[k], START[k] + SIZES[k]
                TT(result[0:Q, a:z, :], ps[0:Q, k, 0:SIZES[k] * F].rearrange("p (c f) -> p c f", f=F),
                   x2_back[0:Q, a:z, :], ALU.add).then_inc(s_res, 1)


_INS = ["x", "src", "dst", "edge_type_4", "L0_gnn_layer_reg", "L1_gnn_W_msg", "L1_gnn_b_msg",
        "L1_gnn_w_ih", "L1_gnn_w_hh", "L1_gnn_b_ih", "L1_gnn_b_hh"]


def kernel(**inputs):
    import numpy as _np
    import concourse.bacc as _bacc
    from concourse import mybir as _mybir
    from concourse.bass_utils import run_bass_kernel_spmd as _run

    nc = _bacc.Bacc("TRN2", target_bir_lowering=False, num_devices=1)
    arrays, args = {}, []
    for name in _INS:
        a = _np.ascontiguousarray(inputs[name])
        arrays[f"in_{name}"] = a
        args.append(nc.dram_tensor(f"in_{name}", a.shape, _mybir.dt.from_np(a.dtype), kind="ExternalInput").ap())
    out = nc.dram_tensor("out_0", (N, F), F32, kind="ExternalOutput").ap()
    build(nc, *args, out)
    r = _run(nc, [arrays], core_ids=[0])
    return r.results[0]["out_0"]
```
